# Optimizing a Trainium2 kernel written in Bass

```python
import numpy as np
import jax
import jax.numpy as jnp

def _softmax(x, axis=-1):
    return jax.nn.softmax(x, axis=axis)
def _gelu(x):
    return jax.nn.gelu(x, approximate=True)
def _silu(x):
    return jax.nn.silu(x)
def _sigmoid(x):
    return jax.nn.sigmoid(x)
def _layernorm(x, axis=-1, eps=1e-5):
    m = jnp.mean(x, axis=axis, keepdims=True)
    v = jnp.var(x, axis=axis, keepdims=True)
    return (x - m) / jnp.sqrt(v + eps)
def _scatter_add(tgt, idx, src, axis=0):
    return tgt.at[idx].add(src)
def _segment_sum(src, seg, n):
    return jax.ops.segment_sum(src, seg, n)

kernel_name = 'mk_metaformer_d1_conv_nhwc128_321da1'

def setup_inputs(seed: int = 0):
    np.random.seed(seed)
    _w = jnp.asarray
    def _rec_inputs():
        import jax
        import jax.numpy as jnp
        _gk = jax.random.key(seed)
        x = -0.000125 + 0.9999 * jax.random.normal(jax.random.fold_in(_gk, 1), (16, 128, 128, 128), jnp.float32)
        return x
    x = _rec_inputs()
    def _L0_conv_setup():
        import jax, jax.numpy as jnp
        import numpy as np
        NUM_HEADS = 8
        EPS = 1e-05

        def _conv1x1(x, w, b):
            return jnp.einsum('bchw,oc->bohw', x, w) + b[None, :, None, None]
        key = jax.random.key(seed)
        ks = jax.random.split(key, 11)
        B, C, H, W = (16, 128, 128, 128)
        std = 0.02
        inp = {'x': jax.random.normal(ks[0], (B, C, H, W), dtype=jnp.float32), 'wq': jax.random.normal(ks[1], (C, C), dtype=jnp.float32) * std, 'bq': jnp.zeros((C,), dtype=jnp.float32), 'wk': jax.random.normal(ks[2], (C, C), dtype=jnp.float32) * std, 'bk': jnp.zeros((C,), dtype=jnp.float32), 'wv': jax.random.normal(ks[3], (C, C), dtype=jnp.float32) * std, 'bv': jnp.zeros((C,), dtype=jnp.float32), 'wo': jax.random.normal(ks[4], (C, C), dtype=jnp.float32) * std, 'bo': jnp.zeros((C,), dtype=jnp.float32), 'gamma': jnp.ones((C,), dtype=jnp.float32), 'beta': jnp.zeros((C,), dtype=jnp.float32)}
        return inp
    _L0_conv_all = _L0_conv_setup()
    _L0_conv_in = {k: v for k, v in _L0_conv_all.items() if k in ('wq', 'bq', 'wk', 'bk', 'wv', 'bv', 'wo', 'bo', 'gamma', 'beta', )}
    del _L0_conv_all

    def _L0_ffn_setup():
        import jax, jax.numpy as jnp
        import numpy as np
        B, S, D, E, H, O, K = (512, 2048, 128, 64, 512, 128, 8)
        key = jax.random.key(seed)
        k0, k1, k2, k3 = jax.random.split(key, 4)
        x = jax.random.normal(k0, (B, S, D), dtype=jnp.float32)
        gate_w = jax.random.normal(k1, (E, D), dtype=jnp.float32) * (1.0 / np.sqrt(D))
        gate_b = jnp.zeros((E,), dtype=jnp.float32)
        weight1 = jax.random.uniform(k2, (E, D + 1, H), dtype=jnp.float32, minval=-1.0, maxval=1.0) * (1.0 / np.sqrt(D + 1))
        weight2 = jax.random.uniform(k3, (E, H + 1, O), dtype=jnp.float32, minval=-1.0, maxval=1.0) * (1.0 / np.sqrt(H + 1))
        return {'x': x, 'gate_w': gate_w, 'gate_b': gate_b, 'weight1': weight1, 'weight2': weight2}
    _L0_ffn_all = _L0_ffn_setup()
    _L0_ffn_in = {k: v for k, v in _L0_ffn_all.items() if k in ('gate_w', 'gate_b', 'weight1', 'weight2', )}
    del _L0_ffn_all

    return {
        "x": x,
        "L0_conv_wq": _L0_conv_in["wq"],
        "L0_conv_bq": _L0_conv_in["bq"],
        "L0_conv_wk": _L0_conv_in["wk"],
        "L0_conv_bk": _L0_conv_in["bk"],
        "L0_conv_wv": _L0_conv_in["wv"],
        "L0_conv_bv": _L0_conv_in["bv"],
        "L0_conv_wo": _L0_conv_in["wo"],
        "L0_conv_bo": _L0_conv_in["bo"],
        "L0_conv_gamma": _L0_conv_in["gamma"],
        "L0_conv_beta": _L0_conv_in["beta"],
        "L0_ffn_gate_w": _L0_ffn_in["gate_w"],
        "L0_ffn_gate_b": _L0_ffn_in["gate_b"],
        "L0_ffn_weight1": _L0_ffn_in["weight1"],
        "L0_ffn_weight2": _L0_ffn_in["weight2"],
    }

def reference(x, L0_conv_wq, L0_conv_bq, L0_conv_wk, L0_conv_bk, L0_conv_wv, L0_conv_bv, L0_conv_wo, L0_conv_bo, L0_conv_gamma, L0_conv_beta, L0_ffn_gate_w, L0_ffn_gate_b, L0_ffn_weight1, L0_ffn_weight2):
    import jax
    import jax.numpy as jnp
    def _L0_conv_ref(x, wq, bq, wk, bk, wv, bv, wo, bo, gamma, beta):
        import jax, jax.numpy as jnp
        import numpy as np
        NUM_HEADS = 8
        EPS = 1e-05

        def _conv1x1(x, w, b):
            return jnp.einsum('bchw,oc->bohw', x, w) + b[None, :, None, None]
        B, C, H, W = x.shape
        nh = NUM_HEADS
        hc = C // nh
        hw = H * W
        q = _conv1x1(x, wq, bq).reshape(B, nh, hc, hw)
        k = _conv1x1(x, wk, bk).reshape(B, nh, hc, hw)
        v = _conv1x1(x, wv, bv).reshape(B, nh, hc, hw)
        scale = hw ** (-0.5)
        attn = jnp.einsum('bhce,bhde->bhcd', q, k) * scale
        attn = jax.nn.softmax(attn, axis=-1)
        out = jnp.einsum('bhcd,bhde->bhce', attn, v).reshape(B, C, H, W)
        out = _conv1x1(out, wo, bo)
        mu = jnp.mean(out, axis=-1, keepdims=True)
        var = jnp.var(out, axis=-1, keepdims=True)
        out = (out - mu) * jax.lax.rsqrt(var + EPS) * gamma + beta
        return out

    def _L0_ffn_ref(x, gate_w, gate_b, weight1, weight2):
        import jax, jax.numpy as jnp
        import numpy as np
        B, S, D, E, H, O, K = (512, 2048, 128, 64, 512, 128, 8)
        Bn, Sn, Dn = x.shape
        logits = jnp.einsum('bsd,ed->bse', x, gate_w) + gate_b
        probs = jax.nn.softmax(logits, axis=1)
        vals, idx = jax.lax.top_k(probs.transpose(0, 2, 1), K)
        topv = vals.transpose(0, 2, 1)
        topi = idx.transpose(0, 2, 1)
        flat_idx = topi.reshape(Bn, K * E)
        gathered = jnp.take_along_axis(x, flat_idx[:, :, None], axis=1)
        gathered = gathered.reshape(Bn, K, E, Dn)
        pooled = jnp.einsum('bked,bke->bed', gathered, topv)
        ones = jnp.ones((E, Bn, 1), dtype=x.dtype)
        h = jnp.concatenate([pooled.transpose(1, 0, 2), ones], axis=-1)
        h = jax.nn.gelu(jnp.einsum('ebd,edh->ebh', h, weight1), approximate=False)
        h = jnp.concatenate([h, ones], axis=-1)
        out = jnp.einsum('ebh,eho->ebo', h, weight2)
        out = out.transpose(1, 0, 2)
        weighted = jnp.einsum('beo,bke->bkeo', out, topv).reshape(Bn, K * E, O)
        outputs = jnp.zeros((Bn, Sn, O), dtype=x.dtype)
        outputs = outputs.at[jnp.arange(Bn)[:, None], flat_idx].add(weighted)
        return outputs

    def _gn(v, G=32, eps=1e-5):
        B_, H_, W_, C_ = v.shape
        g = v.reshape(B_, H_, W_, G, C_ // G)
        m = jnp.mean(g, axis=(1, 2, 4), keepdims=True)
        s = jnp.var(g, axis=(1, 2, 4), keepdims=True)
        return ((g - m) / jnp.sqrt(s + eps)).reshape(v.shape)

    def _ln_c(v, eps=1e-6):
        m = jnp.mean(v, axis=-1, keepdims=True)
        s = jnp.var(v, axis=-1, keepdims=True)
        return (v - m) / jnp.sqrt(s + eps)

    def _ln_t(v, eps=1e-5):
        m = jnp.mean(v, axis=-1, keepdims=True)
        s = jnp.var(v, axis=-1, keepdims=True)
        return (v - m) / jnp.sqrt(s + eps)

    def _to_tokens(v):
        B_, H_, W_, C_ = v.shape
        return v.reshape(B_, H_ * W_, C_)
    def _from_tokens(t, like):
        return t.reshape(like.shape)

    x = x + _L0_conv_ref(_ln_c(x), L0_conv_wq, L0_conv_bq, L0_conv_wk, L0_conv_bk, L0_conv_wv, L0_conv_bv, L0_conv_wo, L0_conv_bo, L0_conv_gamma, L0_conv_beta)
    t = _to_tokens(x)
    t = t + _L0_ffn_ref(_ln_t(t), L0_ffn_gate_w, L0_ffn_gate_b, L0_ffn_weight1, L0_ffn_weight2)
    x = _from_tokens(t, x)
    return x


_drawn_inputs = setup_inputs


def setup_inputs(seed=0):
    import zlib

    import numpy as np

    out = dict(_drawn_inputs(seed))
    spreads = {'L0_conv_bq': (0.0, 0.1),
     'L0_conv_bk': (0.0, 0.1),
     'L0_conv_bv': (0.0, 0.8),
     'L0_conv_bo': (0.0, 0.8),
     'L0_conv_gamma': (1.0, 0.2),
     'L0_conv_beta': (0.0, 0.1),
     'L0_ffn_gate_b': (0.0, 0.1)}
    factors = {'L0_ffn_gate_w': 8.0, 'L0_ffn_weight1': 8.0, 'L0_ffn_weight2': 8.0}
    for name, (base, spread) in spreads.items():
        noise = np.random.default_rng([zlib.crc32(name.encode()), seed]).standard_normal(out[name].shape)
        drawn = base * np.exp(spread * noise) if base else spread * noise
        out[name] = jnp.asarray(drawn.astype(out[name].dtype))
    for name, factor in factors.items():
        out[name] = (out[name] * factor).astype(out[name].dtype)
    return out
```

```python
from contextlib import ExitStack

import concourse.bass as bass
from concourse import mybir

F32 = mybir.dt.float32
U32 = mybir.dt.uint32
ALU = mybir.AluOpType
ACT = mybir.ActivationFunctionType
AX = mybir.AxisListType.X

P = 128
W = 128
TI = 4
NI = P // TI
IC = 4
NK = NI // IC
TC = TI * IC
CW = TC * W
IW = TI * W
XR = 4
NO = 3
HEADS = 8
E = 64
K = 8
EPS_C, EPS_O, EPS_T = 1e-6, 1e-5, 1e-5
SI = 8
NS = NI // SI
SW = SI * TI // 2 * P
HID = 512
HC = HID // P

L_LOAD, L_BNA, L_STA, L_U, L_TRU, L_UT, L_GRAM = 0, 6, 10, 11, 17, 18, 19
S_MUT, S_G, S_A1, S_ATT, S_WP, S_MT = 49, 51, 52, 53, 55, 56
L_MY, L_BNO, L_N, L_GB = 57, 58, 59, 60
L_BNZ, L_STZ, L_STORE = 67, 71, 66
L_TRZ, L_ZT, L_LOG, L_SC, L_TR2, L_LTE = 70, 71, 72, 73, 73, 74
L_MAX, L_MAXI, L_EXP = 82, 86, 87
S_CAND, S_CROSS, S_TOP, S_TEXP, S_FIN = 111, 112, 112, 114, 115


def program(nc, x, wq, bq, wk, bk, wv, wo, gamma, beta, gate_w, gate_b, w1, w2, out):
    NB = x.shape[0]
    HW = x.shape[2] * x.shape[3]
    SCALE = float(HW) ** -0.5
    LOOP0, LOOPS = 4, (NB - 4) // 2
    LAST = NB + (S_FIN + NI - 1) // NI
    x_v = x.rearrange("b c h w -> c b (h w)")
    out_v = out.rearrange("b c h w -> c b (h w)")
    rows_v = out.rearrange("b c h w -> (b c h) w")

    with ExitStack() as ctx:
        def sb(name, shape, dt=F32):
            return ctx.enter_context(nc.sbuf_tensor(name, shape, dt))

        def bank(name):
            return ctx.enter_context(nc.psum_tensor(name, [P, 512], F32))

        def sem(name):
            return ctx.enter_context(nc.semaphore(name))

        U = sb("U", [P, 2, NK, CW])
        xa = sb("xa", [P, XR, CW])
        UT = sb("UT", [P, 2, IW])
        zT = sb("zT", [P, 2, IW])
        Ls = sb("Ls", [P, 2, TI * E])
        LTS = sb("LTS", [P, 2, SW])
        ident = sb("ident", [P, P])
        pick = sb("pick", [P, 2, P])
        gam = sb("gam", [P, W])
        bet = sb("bet", [P, W])
        mask = sb("mask", [P, P])
        nat = sb("nat", [P, 4, P])
        wT = sb("wT", [P, 3, P])
        bqk = sb("bqk", [1, 2, P])
        hbk = sb("hbk", [1, P])
        gwn = LTS[0:E, 0, 0:2 * W].rearrange("p (n w) -> p n w", n=2)
        gws = sb("gws", [E, 2])
        gwT = sb("gwT", [P, E])
        gb2 = sb("gb2", [P, 1])
        stA = sb("stA", [P, 2, TC, 3])
        vA = sb("vA", [P, TC]); sA = sb("sA", [P, TC]); rA = sb("rA", [P, 2, TC])
        MU = sb("MU", [P, 2, P])
        MUT = sb("MUT", [P, 2, P])
        Gs = sb("Gs", [P, P]); A1s = sb("A1s", [P, P]); At = sb("At", [P, P])
        WPs = sb("WPs", [P, P])
        mx = sb("mx", [P, 3])
        MT = sb("MT", [P, 2, P])
        stO = sb("stO", [P, 2, TI, 3])
        vO = sb("vO", [P, 2, TI]); sO = sb("sO", [P, 2, TI]); rO = sb("rO", [P, 2, TI]); mO = sb("mO", [P, 2, TI])
        stZ = sb("stZ", [P, 2, TC, 3])
        vZ = sb("vZ", [P, TC]); sZ = sb("sZ", [P, TC]); rZ = sb("rZ", [P, 2, TC])
        CD = sb("CD", [P, 2, 2 * NS * K + NS])
        CI = sb("CI", [P, 2, NS * K], U32)
        NM = sb("NM", [P, 2, NS])
        ci = sb("ci", [P, 2, NS * K], U32)
        soff = sb("soff", [P, NS * K])
        XV = sb("XV", [P, 2, NS * K]); XT = sb("XT", [P, 2, NS * K]); XS = sb("XS", [P, 2, NS])
        tv = sb("tv", [P, K]); tp = sb("tp", [P, K], U32); tpf = sb("tpf", [P, K]); ng = sb("ng", [P, 1])
        pos = sb("pos", [P, 2 * NS * K])
        hot = sb("hot", [P, K, 2 * NS * K])
        tok8 = sb("tok8", [P, K]); e8 = sb("e8", [P, K]); eL = sb("eL", [P, 2, NS])
        sm = sb("sm", [P, 2 + 2 * NS])
        top8 = sb("top8", [P, K])
        TV = sb("TV", [P, NB * 4])
        TK = sb("TK", [P, NB * 4])

        TKG = sb("TKG", [P, NB * 4], U32)

        room = U[:, :, :, :].rearrange("p a k n -> p (a k n)")
        used = [0]

        def place(*dims, dt=F32, parts=P):
            n = 1
            for d in dims:
                n *= d
            v = room[0:parts, used[0]:used[0] + n]
            used[0] += n
            if dt is not F32:
                v = v.bitcast(dt)
            if len(dims) == 2:
                return v.rearrange("p (a b) -> p a b", a=dims[0])
            if len(dims) == 3:
                return v.rearrange("p (a b c) -> p a b c", a=dims[0], b=dims[1])
            return v

        Q = place(NB, 4 * P, parts=E)
        before = place(4, 4 * P)
        EQ = place(2, 4, 4 * P)
        D = place(2, 4 * P)
        R = place(2, 4, W)
        RC = place(2, 4, W)
        fold = place(E)
        FV = place(2, 4, E)
        FW = place(2, 4, E)
        allone = place(P)
        tvb = place(2, 4); tkb = place(2, 4); wvb = place(2, 4); nfirst = place(2, 4)
        idx = place(2, 4, dt=U32); idxs = place(NB * 4, dt=U32); idxq = place(2, 4, dt=U32)
        boff = place(NB, 4); tkg_f = place(NB * 4)
        stR = place(2, 4, 3); vR = place(2, 4); sR = place(2, 4); rR = place(2, 4)
        junk = place(4 * P)
        sel = place(E, NB, parts=E)
        b1s = place(HID, parts=E); b2s = place(W, parts=E)
        PT = place(E, NB)
        HT = place(2, HC * NB)
        OT = place(NB, E)
        OB = place(2, E); OE = place(2, W, parts=E); QB = place(2, 4 * P, parts=E); C = place(2, 4 * P)
        WR = 8
        wring = xa[:, :, :].rearrange("p a (b n) -> p (a b) n", n=2 * HID)
        w1v = w1.rearrange("e d h -> d e h")
        w2v = w2[:, 0:HID, :].rearrange("e (c p) o -> p e c o", p=P)

        T0, T1, G, LM, LT = (bank(n) for n in ("T0", "T1", "G", "LM", "LT"))
        O = [bank(f"O{i}") for i in range(NO)]
        L, MB = LM[:, 0:TI * E], LM[:, TI * E:512]

        s_const = sem("s_const"); s_iota = sem("s_iota"); s_setup = sem("s_setup"); s_wtp = sem("s_wtp"); s_wtc = sem("s_wtc")
        s_x = [sem(f"s_x{i}") for i in range(XR)]
        s_acc = [sem(f"s_acc{i}") for i in range(2 * NK)]
        s_store = [sem(f"s_store{i}") for i in range(2 * NK)]
        s_setup_dve = sem("s_setup_dve")
        names = ("a_bn a_var a_ln a_rstd a_mu u_ready tru ut_ready gram mut muts g g_copied a1 a1s att att_s "
                 "nmx pexp prs p_ready wp wps mt mt_ready my o_bn o_var o_ln o_r o_rs n_done pool_g gb "
                 "z_bn z_var z_ln z_r trz zt_ready lg l_scaled tr2 lt_done seg_v seg_i seg_nm seg_exp "
                 "tick c1 cand cross crossed t1 t2 texp fin").split()
        S = {n: sem("s_" + n) for n in names}
        s_tail = sem("s_tail"); s_prep = sem("s_prep"); s_bias = sem("s_bias"); s_tkg = sem("s_tkg")
        s_rows = [sem("s_rows0"), sem("s_rows1")]; s_sc = [sem("s_sc0"), sem("s_sc1")]
        s_w = [sem(f"s_w{i}") for i in range(WR)]
        tnames = ("cols idx diag row eq eqn fv qmm q_done cn cnf idxs rbn rvar rln rr cen wv fw pmm p_done "
                  "h ht o ot ob obt oe qb cmm c tick_pe tick_pool").split()
        R_ = {n: sem("r_" + n) for n in tnames}

        def val(b):
            c, it = b
            return c if it is None else it * 2 + c

        def cnt(b, per, extra):
            c, it = b
            base = c * per + extra
            return base if it is None else it * (2 * per) + base

        def item(b, t, lag, per=1):
            c, it = b
            off, i = divmod(t - lag, NI)
            if it is None and not 0 <= c + off < NB:
                return None
            return ((c + off, it), i // per) if i % per == 0 else None

        def wait(eng, s, value):
            if not (isinstance(value, int) and value <= 0):
                eng.wait_ge(s, value)

        def dma_uses(b, extra=0):
            c, it = b
            base = 16 * (c // 2 + 1 + extra)
            return base if it is None else it * 16 + base

        def bodies(eng, body):
            for c in range(LOOP0):
                body((c, None))
            with eng.Fori(0, LOOPS) as it:
                body((LOOP0, it))
                body((LOOP0 + 1, it))
            for c in range(NB, LAST):
                body((c, None))

        def chunk(b, k):
            return U[:, b[0] % 2, k, :]

        def utile(b, i, j):
            o = (i % IC) * IW + j * W
            return U[:, b[0] % 2, i // IC, o:o + W]

        def pair(ap, n):
            return ap[:, 2 * n * W:(2 * n + 2) * W].rearrange("p (h w) -> p w h", h=2)

        NCONST = 16 * 11
        block = ctx.enter_context(nc.Block())

        @block.sync
        def _(sp):
            for i, w in enumerate((wq, wk, wv, wo)):
                sp.dma_start(nat[:, i, :], w).then_inc(s_const, 16)
            sp.dma_start(bqk[:, 0, :], bq.rearrange("(a n) -> a n", a=1)).then_inc(s_const, 16)
            sp.dma_start(bqk[:, 1, :], bk.rearrange("(a n) -> a n", a=1)).then_inc(s_const, 16)
            sp.dma_start(gam[:, :], gamma.rearrange("(a n) -> a n", a=1).to_broadcast([P, W])).then_inc(s_const, 16)
            sp.dma_start(bet[:, :], beta.rearrange("(a n) -> a n", a=1).to_broadcast([P, W])).then_inc(s_const, 16)
            sp.dma_start(gwn[:, 0, :], gate_w).then_inc(s_const, 16)
            for g in range(2):
                sp.dma_start(gb2[g * E:(g + 1) * E, :], gate_b.rearrange("(e a) -> e a", a=1)).then_inc(s_const, 16)

            def body(b):
                for t in range(NI):
                    if r := item(b, t, L_LOAD, IC):
                        a, k = r
                        wait(sp, S["u_ready"], cnt(a, NK, k - XR + 1))
                        bv = val(a)
                        sp.dma_start(xa[:, k % XR:k % XR + 1, :],
                                     x_v[:, bass.ds(bv, 1), k * CW:(k + 1) * CW]).then_inc(s_x[k % XR], 16)
                    if r := item(b, t, L_STORE, IC):
                        a, k = r
                        n = a[0] % 2 * NK + k
                        wait(sp, s_acc[n], dma_uses(a))
                        bv = val(a)
                        sp.dma_start(out_v[:, bass.ds(bv, 1), k * CW:(k + 1) * CW],
                                     U[:, a[0] % 2, k:k + 1, :]).then_inc(s_store[n], 16)

            bodies(sp, body)
            for n in range(2 * NK):
                sp.wait_ge(s_store[n], 16 * (NB // 2))
            sp.sem_inc(s_tail, 1)
            sp.dma_start(b1s, w1[:, W, :]).then_inc(s_bias, 16)
            sp.dma_start(b2s, w2[:, HID, :]).then_inc(s_bias, 16)

            def weights(e, n, s, first):
                if not first:
                    sp.wait_ge(R_["o"], n - WR + 1)
                sp.dma_start(wring[:, s:s + 1, 0:HID], w1v[0:W, bass.ds(e, 1), :]).then_inc(s_w[s], 16)
                sp.dma_start(wring[:, s, HID:2 * HID].rearrange("p (a c o) -> p a c o", a=1, c=HC),
                             w2v[:, bass.ds(e, 1), :, :]).then_inc(s_w[s], 16)

            for s in range(WR):
                weights(s, s, s, True)
            with sp.Fori(1, E // WR) as g:
                for s in range(WR):
                    weights(g * WR + s, g * WR + s, s, False)
            for q in range(2):
                sp.wait_ge(s_sc[q], 64 * (NB // 2))

        @block.gpsimd
        def _(pool):
            gp = nc.gpsimd
            gp.memset(ident[:, :], 0.0).then_inc(s_iota, 1)
            gp.memset(mask[:, :], 0.0).then_inc(s_iota, 1)
            gp.memset(pick[:, :, :], 0.0).then_inc(s_iota, 1)
            pool.wait_ge(s_iota, 3)
            gp.affine_select(out=ident[:, :], in_=ident[:, :], compare_op=ALU.not_equal, fill=1.0, base=0,
                             pattern=[[-1, P]], channel_multiplier=1).then_inc(s_iota, 1)
            hd = P // HEADS
            mv = mask[:, :].rearrange("p (h d) -> p h d", d=hd)
            gp.affine_select(out=mv, in_=mv, compare_op=ALU.is_ge, fill=-1e30, base=0,
                             pattern=[[-hd, HEADS], [0, hd]], channel_multiplier=1).then_inc(s_iota, 1)
            for g in range(2):
                pv = pick[:, g, :].rearrange("p (r e) -> p r e", r=2)
                gp.affine_select(out=pv, in_=pv, compare_op=ALU.not_equal, fill=1.0, base=-g * E,
                                 pattern=[[0, 2], [-1, E]], channel_multiplier=1).then_inc(s_iota, 1)
            pool.wait_ge(s_iota, 7)
            gp.affine_select(out=mv, in_=mv, compare_op=ALU.is_ge, fill=-1e30, base=hd - 1,
                             pattern=[[hd, HEADS], [0, hd]], channel_multiplier=-1).then_inc(s_iota, 1)
            for g in range(2):
                pool.wait_ge(s_iota, 8 + g)
                gp.iota(soff[g * E:(g + 1) * E, :].rearrange("p (s k) -> p s k", k=K),
                        pattern=[[2 * SI * TI // 2, NS], [0, K]], base=g, channel_multiplier=0,
                        allow_small_or_imprecise_dtypes=True).then_inc(s_iota, 1)
            pool.wait_ge(s_iota, 10)
            gp.iota(pos[:, :], pattern=[[1, 2 * NS * K]], base=0, channel_multiplier=0,
                    allow_small_or_imprecise_dtypes=True).then_inc(s_iota, 1)
            pool.wait_ge(s_const, NCONST)

            gam_b = gam[:, :].unsqueeze(1).to_broadcast([P, 2 * TI, W])
            bet_b = bet[:, :].unsqueeze(1).to_broadcast([P, 2 * TI, W])

            def body(b):
                for t in range(NI):
                    if r := item(b, t, L_U, IC):
                        a, k = r
                        pool.wait_ge(S["a_rstd"], cnt(a, NK, k + 1))
                        wait(pool, S["trz"], cnt(a, NI, IC * k + IC - 2 * NI))
                        wait(pool, s_store[a[0] % 2 * NK + k], dma_uses(a, -1))
                        gp.tensor_tensor(chunk(a, k).rearrange("p (h w) -> p h w", w=W),
                                         xa[:, k % XR, :].rearrange("p (h w) -> p h w", w=W),
                                         rA[:, k % 2, :].unsqueeze(2).to_broadcast([P, TC, W]),
                                         ALU.mult).then_inc(S["u_ready"], 1)
                    if r := item(b, t, L_GB):
                        a, i = r
                        if i % 2 == 1:
                            p = i // 2
                            pool.wait_ge(S["n_done"], cnt(a, NI, i + 1))
                            o = p % 2 * 2 * IW
                            v = chunk(a, i // IC)[:, o:o + 2 * IW].rearrange("p (h w) -> p h w", w=W)
                            gp.tensor_tensor(v, v, gam_b, ALU.mult).then_inc(S["pool_g"], 1)
                            pool.wait_ge(S["pool_g"], cnt(a, NI // 2, p + 1))
                            gp.tensor_tensor(v, v, bet_b, ALU.add).then_inc(S["gb"], 1)
                            if p % 2 == 1:
                                k = i // IC
                                pool.wait_ge(S["gb"], cnt(a, NI // 2, p + 1))
                                bv = val(a)
                                gp.dma_start(U[:, a[0] % 2, k:k + 1, :],
                                             x_v[:, bass.ds(bv, 1), k * CW:(k + 1) * CW],
                                             accum_op=ALU.add).then_inc(s_acc[a[0] % 2 * NK + k], 16)

            bodies(pool, body)
            pool.wait_ge(s_tail, 1)
            gp.memset(before, 1.0).then_inc(s_prep, 1)
            gp.memset(sel, 0.0).then_inc(s_prep, 1)
            gp.memset(allone, 1.0).then_inc(s_prep, 1)
            pool.wait_ge(s_prep, 3)
            gp.iota(boff, pattern=[[HW // W * P // P * W, NB], [0, 4]], base=0, channel_multiplier=0,
                    allow_small_or_imprecise_dtypes=True).then_inc(s_prep, 1)
            gp.affine_select(out=sel, in_=sel, compare_op=ALU.not_equal, fill=1.0, base=0,
                             pattern=[[-1, E], [0, NB]], channel_multiplier=1).then_inc(s_prep, 1)
            for j in range(4):
                gp.affine_select(out=before[:, j, :], in_=before[:, j, :], compare_op=ALU.is_gt, fill=0.0,
                                 base=P * j, pattern=[[-1, 4 * P]], channel_multiplier=1).then_inc(s_prep, 1)

            with pool.Fori(0, NB // 2) as g:
                for q in range(2):
                    n = g * 2 + q
                    pool.wait_ge(R_["idx"], n + 1)
                    pool.sem_inc(R_["tick_pool"], 1)
                    for j in range(4):
                        gp.indirect_dma_start(out=R[:, q, j, :], out_offset=None, in_=rows_v,
                                              in_offset=bass.IndirectOffsetOnAxis(ap=idx[:, q, j:j + 1], axis=0),
                                              ).then_inc(s_rows[q], 16)
            with pool.Fori(0, NB // 2) as g:
                for q in range(2):
                    n = g * 2 + q
                    pool.wait_ge(R_["c"], n + 1)
                    pool.sem_inc(R_["tick_pool"], 1)
                    for j in range(4):
                        gp.indirect_dma_start(out=rows_v,
                                              out_offset=bass.IndirectOffsetOnAxis(ap=idxq[:, q, j:j + 1], axis=0),
                                              in_=C[:, q, j * P:(j + 1) * P], in_offset=None,
                                              bounds_check=NB * P * P - 1, oob_is_err=False,
                                              compute_op=ALU.add).then_inc(s_sc[q], 16)

        @block.scalar
        def _(act):
            sc = nc.scalar
            sc.preload_act_table_set("natural_log_exp_and_others")

            def body(b):
                for t in range(NI):
                    if r := item(b, t, L_UT):
                        a, i = r
                        act.wait_ge(S["tru"], cnt(a, NI, i + 1))
                        wait(act, S["gram"], cnt(a, NI, i - 1))
                        sc.activation(UT[:, i % 2, :], T0[:, :], ACT.Copy).then_inc(S["ut_ready"], 1)
                    if r := item(b, t, L_ZT):
                        a, i = r
                        act.wait_ge(S["trz"], cnt(a, NI, i + 1))
                        wait(act, S["lg"], cnt(a, NI, i - 1))
                        sc.activation(zT[:, i % 2, :], T1[:, :], ACT.Copy).then_inc(S["zt_ready"], 1)
                    if r := item(b, t, L_BNO):
                        a, i = r
                        act.wait_ge(S["o_var"], cnt(a, NI, i + 1))
                        sc.activation(sO[:, i % 2, :], vO[:, i % 2, :], ACT.Ln).then_inc(S["o_ln"], 1)
                        act.wait_ge(S["o_ln"], cnt(a, NI, i + 1))
                        sc.activation(rO[:, i % 2, :], sO[:, i % 2, :], ACT.Exp, scale=-0.5).then_inc(S["o_r"], 1)
                    if r := item(b, t, L_LTE):
                        a, i = r
                        act.wait_ge(S["tr2"], cnt(a, NI, i + 1))
                        s = i // SI
                        if i % SI == 0:
                            wait(act, S["seg_exp"], cnt(a, NS, s - 1))
                        o = i % SI * TI * E
                        sc.activation(LTS[:, s % 2, o:o + TI * E], LT[:, 0:TI * E], ACT.Identity,
                                      bias=gb2[:, 0:1]).then_inc(S["lt_done"], 1)
                    if r := item(b, t, L_N):
                        a, i = r
                        act.wait_ge(S["o_rs"], cnt(a, NI, i + 1))
                        for j in range(TI):
                            last = sc.activation(utile(a, i, j), O[i % NO][:, j * W:(j + 1) * W], ACT.Identity,
                                                 scale=rO[:, i % 2, j:j + 1], bias=mO[:, i % 2, j:j + 1])
                        last.then_inc(S["n_done"], 1)
                    if r := item(b, t, L_STA, IC):
                        a, k = r
                        act.wait_ge(S["a_var"], cnt(a, NK, k + 1))
                        sc.activation(sA[:, :], vA[:, :], ACT.Ln).then_inc(S["a_ln"], 1)
                        act.wait_ge(S["a_ln"], cnt(a, NK, k + 1))
                        sc.activation(rA[:, k % 2, :], sA[:, :], ACT.Exp, scale=-0.5).then_inc(S["a_rstd"], 1)
                    if r := item(b, t, L_STZ, IC):
                        a, k = r
                        act.wait_ge(S["z_var"], cnt(a, NK, k + 1))
                        sc.activation(sZ[:, :], vZ[:, :], ACT.Ln).then_inc(S["z_ln"], 1)
                        act.wait_ge(S["z_ln"], cnt(a, NK, k + 1))
                        sc.activation(rZ[:, k % 2, :], sZ[:, :], ACT.Exp, scale=-0.5).then_inc(S["z_r"], 1)
                    if r := item(b, t, L_EXP, SI):
                        a, s = r
                        act.wait_ge(S["seg_nm"], cnt(a, NS, s + 1))
                        sc.activation(LTS[:, s % 2, :], LTS[:, s % 2, :], ACT.Exp, bias=NM[:, a[0] % 2, s:s + 1],
                                      accum_out=CD[:, a[0] % 2, 2 * NS * K + s:2 * NS * K + s + 1]).then_inc(S["seg_exp"], 1)
                    if (r := item(b, t, S_ATT, NI)):
                        a, _ = r
                        act.wait_ge(S["nmx"], cnt(a, 1, 1))
                        sc.activation(At[:, :], At[:, :], ACT.Exp, bias=mx[:, 0:1],
                                      accum_out=mx[:, 1:2]).then_inc(S["pexp"], 1)
                    if (r := item(b, t, S_TEXP, NI)):
                        a, _ = r
                        act.wait_ge(S["t1"], cnt(a, 4, 4))
                        sc.activation(e8[:, :], tv[:, :], ACT.Exp, bias=ng[:, 0:1])
                        sc.activation(eL[:, :, :], XV[:, :, 0:NS * K:K], ACT.Exp, bias=ng[:, 0:1]).then_inc(S["texp"], 1)

            bodies(act, body)

            with act.Fori(0, NB // 2) as g:
                for q in range(2):
                    n = g * 2 + q
                    act.wait_ge(R_["rvar"], n + 1)
                    sc.activation(sR[:, q, :], vR[:, q, :], ACT.Ln).then_inc(R_["rln"], 1)
                    act.wait_ge(R_["rln"], n + 1)
                    sc.activation(rR[:, q, :], sR[:, q, :], ACT.Exp, scale=-0.5).then_inc(R_["rr"], 1)
                    act.wait_ge(R_["qmm"], n + 1)
                    sc.activation(Q[:, bass.ds(n, 1), :], O[q][0:E, :].unsqueeze(1), ACT.Copy).then_inc(R_["q_done"], 1)
                    act.wait_ge(R_["pmm"], n + 1)
                    sc.activation(PT[:, :, bass.ds(n, 1)], (L, LT)[q][:, 0:E].unsqueeze(2), ACT.Copy).then_inc(R_["p_done"], 1)
            with act.Fori(0, E // 2) as g:
                for q in range(2):
                    n = g * 2 + q
                    act.wait_ge(R_["h"], n + 1)
                    sc.activation(HT[:, q, :], (G, O[2])[q][:, 0:HC * NB], ACT.Gelu).then_inc(R_["ht"], 1)
            with act.Fori(0, NB // 2) as g:
                for q in range(2):
                    n = g * 2 + q
                    act.wait_ge(R_["cmm"], n + 1)
                    act.wait_ge(R_["qb"], n + 1)
                    sc.activation(C[:, q, :], O[q][:, :], ACT.Copy).then_inc(R_["c"], 1)

        @block.tensor
        def _(pe):
            te = nc.tensor
            pe.wait_ge(s_iota, 7)
            pe.wait_ge(s_const, NCONST)
            for n, i in enumerate((0, 1, 3)):
                last = te.transpose(T0[:, n * P:(n + 1) * P], nat[:, i, :], ident[:, :])
            last.then_inc(s_wtp, 1)
            pe.wait_ge(s_setup, 1)
            te.transpose(L[:, 0:E], gwn[:, 1, :], ident[0:E, 0:E]).then_inc(s_wtp, 1)
            pe.wait_ge(s_wtc, 2)

            def product(a, i):
                if i == 0:
                    pe.wait_ge(S["mt_ready"], cnt(a, 1, 1))
                wait(pe, S["n_done"], cnt(a, NI, i - NO + 1 if i >= NO else i - 1))
                o = i % IC * IW
                te.matmul(O[i % NO][:, :], MT[:, a[0] % 2, :], chunk(a, i // IC)[:, o:o + IW],
                          start=True, stop=True).then_inc(S["my"], 1)

            def body(b):
                for t in range(NI):
                    if (r := item(b, t, L_MY)) and r[1] >= 2:
                        product(*r)
                    if r := item(b, t, L_GRAM):
                        a, i = r
                        pe.wait_ge(S["ut_ready"], cnt(a, NI, i + 1))
                        if i == 0:
                            wait(pe, S["g_copied"], cnt(a, 1, 0))
                        for j in range(TI):
                            v = UT[:, i % 2, j * W:(j + 1) * W]
                            last = te.matmul(G[:, 0:P], v, v, start=(i == 0 and j == 0), stop=False)
                        last.then_inc(S["gram"], 1)
                        if i == NI - 1:
                            pe.wait_ge(S["muts"], cnt(a, 1, 1))
                            te.matmul(G[:, 0:P], MUT[:, 1, :], MUT[:, 0, :], start=False, stop=True).then_inc(S["g"], 1)
                    if any(item(b, t, stage, NI) for stage in (S_CROSS, S_MUT, S_A1, S_ATT, S_WP, S_MT)):
                        if r := item(b, t - 1, L_LOG):
                            pe.wait_ge(S["l_scaled"], cnt(r[0], NI, r[1] + 1))
                    if (r := item(b, t, S_CROSS, NI)):
                        a, _ = r
                        pe.wait_ge(S["cand"], cnt(a, 1, 1))
                        pe.wait_ge(S["seg_exp"], cnt(a, NS, NS))
                        c, it = a
                        pe.wait_ge(S["mt_ready"], cnt(a, 1, 2 if it is not None else min(2, NB - c)))
                        n = 2 * NS * K + NS
                        for g in range(2):
                            last = te.matmul(MB[:, g * n:(g + 1) * n], pick[:, g, :], CD[:, a[0] % 2, :], start=True, stop=True)
                        last.then_inc(S["cross"], 1)
                    if (r := item(b, t, S_MUT, NI)):
                        a, _ = r
                        pe.wait_ge(S["a_mu"], cnt(a, NK, NK))
                        wait(pe, S["crossed"], cnt(a, 1, -1))
                        wait(pe, S["mt_ready"], cnt(a, 1, 0))
                        te.transpose(MB[:, 0:P], MU[:, a[0] % 2, :], ident[:, :]).then_inc(S["mut"], 1)
                    if (r := item(b, t, S_A1, NI)):
                        a, _ = r
                        pe.wait_ge(S["g_copied"], cnt(a, 1, 1))
                        te.matmul(MB[:, 0:P], Gs[:, :], wT[:, 1, :], start=True, stop=True).then_inc(S["a1"], 1)
                    if (r := item(b, t, S_ATT, NI)):
                        a, _ = r
                        pe.wait_ge(S["a1s"], cnt(a, 1, 1))
                        te.matmul(MB[:, 0:P], wT[:, 0, :], A1s[:, :], start=True, stop=False)
                        te.matmul(MB[:, 0:P], bqk[:, 0, :], hbk[:, :], start=False, stop=True).then_inc(S["att"], 1)
                    if (r := item(b, t, S_WP, NI)):
                        a, _ = r
                        pe.wait_ge(S["p_ready"], cnt(a, 1, 1))
                        te.matmul(MB[:, 0:P], At[:, :], wT[:, 2, :], start=True, stop=True).then_inc(S["wp"], 1)
                    if (r := item(b, t, S_MT, NI)):
                        a, _ = r
                        pe.wait_ge(S["wps"], cnt(a, 1, 1))
                        te.matmul(MB[:, 0:P], nat[:, 2, :], WPs[:, :], start=True, stop=True).then_inc(S["mt"], 1)
                    if r := item(b, t, L_TRU):
                        a, i = r
                        if i % IC == 0:
                            pe.wait_ge(S["u_ready"], cnt(a, NK, i // IC + 1))
                        wait(pe, S["ut_ready"], cnt(a, NI, i))
                        for j in range(TI):
                            last = te.transpose(T0[:, j * W:(j + 1) * W], utile(a, i, j), ident[:, :])
                        last.then_inc(S["tru"], 1)
                    if r := item(b, t, L_TR2):
                        a, i = r
                        pe.wait_ge(S["l_scaled"], cnt(a, NI, i + 1))
                        wait(pe, S["lt_done"], cnt(a, NI, i))
                        for j in range(TI // 2):
                            last = te.transpose(LT[:, j * P:(j + 1) * P], Ls[:, i % 2, j * P:(j + 1) * P], ident[:, :])
                        last.then_inc(S["tr2"], 1)
                    if r := item(b, t, L_LOG):
                        a, i = r
                        pe.wait_ge(S["zt_ready"], cnt(a, NI, i + 1))
                        wait(pe, S["l_scaled"], cnt(a, NI, i))
                        for stage, read in ((S_CROSS, "crossed"), (S_MUT, "muts"), (S_A1, "a1s"), (S_ATT, "att_s"),
                                            (S_WP, "wps"), (S_MT, "mt_ready")):
                            if m := item(b, t, stage, NI):
                                pe.wait_ge(S[read], cnt(m[0], 1, 1))
                        for j in range(TI):
                            last = te.matmul(L[:, j * E:(j + 1) * E], zT[:, i % 2, j * W:(j + 1) * W], gwT[:, :],
                                             start=True, stop=True)
                        last.then_inc(S["lg"], 1)
                    if r := item(b, t, L_TRZ):
                        a, i = r
                        if i % IC == 0:
                            pe.wait_ge(s_acc[a[0] % 2 * NK + i // IC], dma_uses(a))
                        wait(pe, S["zt_ready"], cnt(a, NI, i))
                        for j in range(TI):
                            last = te.transpose(T1[:, j * W:(j + 1) * W], utile(a, i, j), ident[:, :])
                        last.then_inc(S["trz"], 1)
                    if (r := item(b, t, L_MY)) and r[1] < 2:
                        product(*r)

            bodies(pe, body)
            pe.wait_ge(s_prep, 9)
            pe.wait_ge(s_bias, 32)

            with pe.Fori(0, NB // 2) as g:
                for q in range(2):
                    n = g * 2 + q
                    pe.wait_ge(R_["diag"], n + 1)
                    te.matmul((T0, T1)[q][:, :], allone, D[:, q, :], start=True, stop=True).then_inc(R_["row"], 1)
                    pe.wait_ge(R_["fv"], n + 1)
                    for j in range(4):
                        last = te.matmul(O[q][0:E, :], FV[:, q, j, :], EQ[:, q, j, :], start=(j == 0), stop=(j == 3))
                    last.then_inc(R_["qmm"], 1)
                    pe.wait_ge(R_["fw"], n + 1)
                    for j in range(4):
                        last = te.matmul((L, LT)[q][:, 0:E], RC[:, q, j, :], FW[:, q, j, :], start=(j == 0), stop=(j == 3))
                    last.then_inc(R_["pmm"], 1)
            pe.wait_ge(R_["p_done"], NB)

            def experts(g):
                for s in range(WR):
                    q = s % 2
                    n = g * WR + s
                    pe.wait_ge(s_w[s], g * 32 + 32)
                    for c in range(HC):
                        h = (G, O[2])[q][:, c * NB:(c + 1) * NB]
                        te.matmul(h, wring[:, s, c * P:(c + 1) * P], PT[:, bass.ds(n, 1), :], start=True, stop=False)
                        last = te.matmul(h, b1s[:, c * P:(c + 1) * P], sel[:, bass.ds(n, 1), :], start=False, stop=True)
                    last.then_inc(R_["h"], 1)
                    pe.wait_ge(R_["ht"], n + 1)
                    wait(pe, R_["ot"], n - 1)
                    for c in range(HC):
                        te.matmul((T0, T1)[q][:, 0:NB], wring[:, s, HID + c * P:HID + (c + 1) * P],
                                  HT[:, q, c * NB:(c + 1) * NB], start=(c == 0), stop=False)
                    te.matmul((T0, T1)[q][:, 0:NB], b2s, sel[:, bass.ds(n, 1), :], start=False, stop=True).then_inc(R_["o"], 1)

            experts(0)
            with pe.Fori(1, E // WR) as g:
                experts(g)
            with pe.Fori(0, NB // 2) as g:
                for q in range(2):
                    n = g * 2 + q
                    pe.wait_ge(R_["ob"], n + 1)
                    pe.sem_inc(R_["tick_pe"], 1)
                    te.transpose((T0, T1)[q][0:E, 0:P], OB[:, q, :], ident[:, :]).then_inc(R_["obt"], 1)
                    pe.wait_ge(R_["qb"], n + 1)
                    for j in range(4):
                        last = te.matmul(O[q][:, j * P:(j + 1) * P], QB[:, q, j * P:(j + 1) * P], OE[:, q, :],
                                         start=True, stop=True)
                    last.then_inc(R_["cmm"], 1)

        @block.vector
        def _(dve):
            ve = nc.vector
            dve.wait_ge(s_const, NCONST)
            chain = [0]

            def link(ins):
                chain[0] += 1
                ins.then_inc(s_setup_dve, 1)
                dve.wait_ge(s_setup_dve, chain[0])

            link(ve.tensor_scalar(hbk[:, :], bqk[:, 1, :], float(HW), None, ALU.mult))
            link(ve.tensor_reduce(gws[:, 0:1], gwn[:, 0, :], AX, ALU.add))
            link(ve.tensor_scalar(gws[:, 1:2], gws[:, 0:1], 1.0 / W, None, ALU.mult))
            ve.tensor_scalar(gwn[:, 1, :], gwn[:, 0, :], gws[:, 1:2], None, ALU.subtract).then_inc(s_setup, 1)
            dve.wait_ge(s_wtp, 1)
            ve.tensor_copy(wT[:, :, :], T0[:, 0:3 * P].rearrange("p (n f) -> p n f", n=3)).then_inc(s_wtc, 1)
            dve.wait_ge(s_wtp, 2)
            ve.tensor_copy(gwT[:, :], L[:, 0:E]).then_inc(s_wtc, 1)
            dve.wait_ge(s_iota, 11)

            def body(b):
                for t in range(NI):
                    if (r := item(b, t, S_G, NI)):
                        a, _ = r
                        dve.wait_ge(S["g"], cnt(a, 1, 1))
                        ve.tensor_copy(Gs[:, :], G[:, 0:P]).then_inc(S["g_copied"], 1)
                    if r := item(b, t, L_BNO):
                        a, i = r
                        dve.wait_ge(S["my"], cnt(a, NI, i + 1))
                        for n in range(TI // 2):
                            last = ve.bn_stats(stO[:, i % 2, 2 * n:2 * n + 2, :].rearrange("p n s -> p (n s)"), pair(O[i % NO], n))
                        last.then_inc(S["o_bn"], 1)
                        dve.wait_ge(S["o_bn"], cnt(a, NI, i + 1))
                        ve.tensor_scalar(vO[:, i % 2, :], stO[:, i % 2, :, 2], 1.0 / W, EPS_O, ALU.mult, ALU.add).then_inc(S["o_var"], 1)
                    if r := item(b, t, L_SC):
                        a, i = r
                        dve.wait_ge(S["lg"], cnt(a, NI, i + 1))
                        wait(dve, S["tr2"], cnt(a, NI, i - 1))
                        ve.tensor_tensor(Ls[:, i % 2, :].rearrange("p (h e) -> p h e", e=E),
                                         L[:, 0:TI * E].rearrange("p (h e) -> p h e", e=E),
                                         rZ[:, i // IC % 2, i % IC * TI:(i % IC + 1) * TI].unsqueeze(2).to_broadcast([P, TI, E]),
                                         ALU.mult).then_inc(S["l_scaled"], 1)
                    if (r := item(b, t, S_TOP, NI)):
                        a, _ = r
                        dve.wait_ge(S["cross"], cnt(a, 1, 1))
                        n = 2 * NS * K + NS
                        mv = MB[:, 0:2 * n].rearrange("p (g n) -> p g n", g=2)
                        ve.tensor_copy(XV[:, :, :], mv[:, :, 0:NS * K])
                        ve.tensor_copy(XT[:, :, :], mv[:, :, NS * K:2 * NS * K])
                        ve.tensor_copy(XS[:, :, :], mv[:, :, 2 * NS * K:n]).then_inc(S["crossed"], 1)
                        dve.wait_ge(S["crossed"], cnt(a, 1, 1))
                        xv = XV[:, :, :].rearrange("p g n -> p (g n)")
                        dve.sem_inc(S["tick"], 1)
                        ve.max(tv[:, :], xv).then_inc(S["t1"], 1)
                        dve.wait_ge(S["t1"], cnt(a, 4, 1))
                        ve.tensor_scalar(ng[:, :], tv[:, 0:1], -1.0, None, ALU.mult)
                        dve.sem_inc(S["tick"], 1)
                        ve.max_index(tp[:, :], tv[:, :], xv).then_inc(S["t1"], 1)
                        dve.wait_ge(S["t1"], cnt(a, 4, 2))
                        ve.tensor_copy(tpf[:, :], tp[:, :]).then_inc(S["t1"], 1)
                        dve.wait_ge(S["t1"], cnt(a, 4, 3))
                        M = 2 * NS * K
                        ve.tensor_tensor(hot[:, :, :], pos[:, :].unsqueeze(1).to_broadcast([P, K, M]),
                                         tpf[:, :].unsqueeze(2).to_broadcast([P, K, M]), ALU.is_equal).then_inc(S["t1"], 1)
                    if (r := item(b, t, S_MUT, NI)):
                        a, _ = r
                        dve.wait_ge(S["mut"], cnt(a, 1, 1))
                        ve.tensor_copy(MUT[:, 0, :], MB[:, 0:P])
                        ve.tensor_scalar(MUT[:, 1, :], MB[:, 0:P], -float(W), None, ALU.mult).then_inc(S["muts"], 1)
                    if (r := item(b, t, S_A1, NI)):
                        a, _ = r
                        dve.wait_ge(S["a1"], cnt(a, 1, 1))
                        ve.tensor_copy(A1s[:, :], MB[:, 0:P]).then_inc(S["a1s"], 1)
                    if (r := item(b, t, S_ATT, NI)):
                        a, _ = r
                        dve.wait_ge(S["att"], cnt(a, 1, 1))
                        ve.scalar_tensor_tensor(At[:, :], MB[:, 0:P], SCALE, mask[:, :], ALU.mult, ALU.add).then_inc(S["att_s"], 1)
                        dve.wait_ge(S["att_s"], cnt(a, 1, 1))
                        ve.tensor_reduce(mx[:, 0:1], At[:, :], AX, ALU.max, negate=True).then_inc(S["nmx"], 1)
                    if (r := item(b, t, S_ATT + 1, NI)):
                        a, _ = r
                        dve.wait_ge(S["pexp"], cnt(a, 1, 1))
                        ve.reciprocal(mx[:, 2:3], mx[:, 1:2]).then_inc(S["prs"], 1)
                        dve.wait_ge(S["prs"], cnt(a, 1, 1))
                        ve.tensor_scalar(At[:, :], At[:, :], mx[:, 2:3], None, ALU.mult).then_inc(S["p_ready"], 1)
                    if (r := item(b, t, S_WP, NI)):
                        a, _ = r
                        dve.wait_ge(S["wp"], cnt(a, 1, 1))
                        ve.tensor_copy(WPs[:, :], MB[:, 0:P]).then_inc(S["wps"], 1)
                    if (r := item(b, t, S_MT, NI)):
                        a, _ = r
                        dve.wait_ge(S["mt"], cnt(a, 1, 1))
                        ve.tensor_copy(MT[:, a[0] % 2, :], MB[:, 0:P]).then_inc(S["mt_ready"], 1)
                    if r := item(b, t, L_STA + 1, IC):
                        a, k = r
                        dve.wait_ge(S["a_rstd"], cnt(a, NK, k + 1))
                        ve.tensor_tensor(MU[:, a[0] % 2, k * TC:(k + 1) * TC], stA[:, k % 2, :, 1], rA[:, k % 2, :], ALU.mult).then_inc(S["a_mu"], 1)
                    if r := item(b, t, L_STZ + 1, IC):
                        a, k = r
                        dve.wait_ge(S["z_r"], cnt(a, NK, k + 1))
                    if r := item(b, t, L_BNA):
                        a, i = r
                        k = i // IC
                        if i % IC == 0:
                            c, it = a
                            base = 16 * (2 * c + k // XR + 1)
                            dve.wait_ge(s_x[k % XR], base if it is None else it * 64 + base)
                            wait(dve, S["a_mu"], cnt(a, NK, k - 1))
                        for n in range(TI // 2):
                            j = i % IC * TI + 2 * n
                            last = ve.bn_stats(stA[:, k % 2, j:j + 2, :].rearrange("p n s -> p (n s)"), pair(xa[:, k % XR, :], j // 2))
                        last.then_inc(S["a_bn"], 1)
                    if r := item(b, t, L_STA, IC):
                        a, k = r
                        dve.wait_ge(S["a_bn"], cnt(a, NI, IC * k + IC))
                        wait(dve, S["u_ready"], cnt(a, NK, k - 1))
                        ve.tensor_scalar(vA[:, :], stA[:, k % 2, :, 2], 1.0 / W, EPS_C, ALU.mult, ALU.add).then_inc(S["a_var"], 1)
                    if r := item(b, t, L_BNO):
                        a, i = r
                        dve.wait_ge(S["o_r"], cnt(a, NI, i + 1))
                        ve.scalar_tensor_tensor(mO[:, i % 2, :], stO[:, i % 2, :, 1], -1.0, rO[:, i % 2, :], ALU.mult, ALU.mult).then_inc(S["o_rs"], 1)
                    if r := item(b, t, L_BNZ):
                        a, i = r
                        k = i // IC
                        if i % IC == 0:
                            dve.wait_ge(s_acc[a[0] % 2 * NK + k], dma_uses(a))
                        for n in range(TI // 2):
                            j = i % IC * TI + 2 * n
                            last = ve.bn_stats(stZ[:, k % 2, j:j + 2, :].rearrange("p n s -> p (n s)"), pair(chunk(a, k), j // 2))
                        last.then_inc(S["z_bn"], 1)
                    if r := item(b, t, L_STZ, IC):
                        a, k = r
                        dve.wait_ge(S["z_bn"], cnt(a, NI, IC * k + IC))
                        ve.tensor_scalar(vZ[:, :], stZ[:, k % 2, :, 2], 1.0 / W, EPS_T, ALU.mult, ALU.add).then_inc(S["z_var"], 1)
                    if r := item(b, t, L_MAX, SI):
                        a, s = r
                        q = a[0] % 2
                        dve.wait_ge(S["lt_done"], cnt(a, NI, SI * s + SI))
                        if s == 0:
                            wait(dve, S["cross"], cnt(a, 1, -1))
                        dve.sem_inc(S["tick"], 1)
                        ve.max(CD[:, q, s * K:(s + 1) * K], LTS[:, s % 2, :]).then_inc(S["seg_v"], 1)
                    if (r := item(b, t, L_MAXI, SI)):
                        a, s = r
                        q = a[0] % 2
                        dve.wait_ge(S["seg_v"], cnt(a, NS, s + 1))
                        dve.sem_inc(S["tick"], 1)
                        ve.max_index(CI[:, q, s * K:(s + 1) * K], CD[:, q, s * K:(s + 1) * K], LTS[:, s % 2, :]).then_inc(S["seg_i"], 1)
                        ve.tensor_scalar(NM[:, q, s:s + 1], CD[:, q, s * K:s * K + 1], -1.0, None, ALU.mult).then_inc(S["seg_nm"], 1)
                    if (r := item(b, t, S_CAND, NI)):
                        a, _ = r
                        q = a[0] % 2
                        dve.wait_ge(S["seg_i"], cnt(a, NS, NS))
                        ve.tensor_scalar(ci[:, 0, :], CI[:, q, :], P - 1, 7, ALU.bitwise_and, ALU.logical_shift_left)
                        ve.tensor_scalar(ci[:, 1, :], CI[:, q, :], 7, 1, ALU.logical_shift_right, ALU.logical_shift_left).then_inc(S["c1"], 1)
                        dve.wait_ge(S["c1"], cnt(a, 2, 1))
                        tk = CD[:, q, NS * K:2 * NS * K]
                        ve.tensor_tensor(tk, ci[:, 0, :], ci[:, 1, :], ALU.add).then_inc(S["c1"], 1)
                        dve.wait_ge(S["c1"], cnt(a, 2, 2))
                        ve.tensor_tensor(tk, tk, soff[:, :], ALU.add).then_inc(S["cand"], 1)
                    if (r := item(b, t, S_TOP + 1, NI)):
                        a, _ = r
                        M = 2 * NS * K
                        dve.wait_ge(S["t1"], cnt(a, 4, 4))
                        xt = XT[:, :, :].rearrange("p g n -> p (g n)").unsqueeze(1).to_broadcast([P, K, M])
                        ve.tensor_tensor(hot[:, :, :], hot[:, :, :], xt, ALU.mult).then_inc(S["t2"], 1)
                        dve.wait_ge(S["t2"], cnt(a, 5, 1))
                        ve.tensor_reduce(tok8[:, :], hot[:, :, :], AX, ALU.add).then_inc(S["t2"], 1)
                    if (r := item(b, t, S_FIN, NI)):
                        a, _ = r
                        dve.wait_ge(S["texp"], cnt(a, 1, 1))
                        ve.tensor_tensor(sm[:, 2:2 + 2 * NS], eL[:, :, :].rearrange("p g n -> p (g n)"),
                                         XS[:, :, :].rearrange("p g n -> p (g n)"), ALU.mult).then_inc(S["t2"], 1)
                        dve.wait_ge(S["t2"], cnt(a, 5, 3))
                        ve.tensor_reduce(sm[:, 0:1], sm[:, 2:2 + 2 * NS], AX, ALU.add).then_inc(S["t2"], 1)
                        dve.wait_ge(S["t2"], cnt(a, 5, 4))
                        ve.reciprocal(sm[:, 1:2], sm[:, 0:1]).then_inc(S["t2"], 1)
                        dve.wait_ge(S["t2"], cnt(a, 5, 5))
                        bv = val(a)
                        for g in range(2):
                            h = slice(g * E, (g + 1) * E)
                            ve.tensor_scalar(TV[h, bass.ds(bv * 4, 4)], e8[h, g * 4:g * 4 + 4], sm[h, 1:2], None, ALU.mult)
                            last = ve.tensor_copy(TK[h, bass.ds(bv * 4, 4)], tok8[h, g * 4:g * 4 + 4])
                        last.then_inc(S["fin"], 1)

            bodies(dve, body)
            dve.wait_ge(s_tail, 1)
            dve.wait_ge(s_prep, 9)
            ve.tensor_tensor(fold, ident[:, 0:E], ident[:, E:2 * E], ALU.add).then_inc(s_tkg, 1)
            dve.wait_ge(S["fin"], NB)
            ve.tensor_tensor(tkg_f, TK[:, :], boff.rearrange("p a b -> p (a b)"), ALU.add).then_inc(s_tkg, 1)
            dve.wait_ge(s_tkg, 2)
            ve.tensor_copy(TKG[:, :], tkg_f).then_inc(s_tkg, 1)
            dve.wait_ge(s_tkg, 3)

            with dve.Fori(0, NB // 2) as g:
                for q in range(2):
                    n = g * 2 + q
                    ve.tensor_copy(tvb[:, q, :], TV[:, bass.ds(n * 4, 4)])
                    ve.tensor_copy(tkb[:, q, :], TK[:, bass.ds(n * 4, 4)]).then_inc(R_["cols"], 1)
                    ve.tensor_copy(idx[:, q, :], TKG[:, bass.ds(n * 4, 4)]).then_inc(R_["idx"], 1)
                    dve.wait_ge(R_["cols"], n + 1)
                    for j in range(4):
                        last = ve.tensor_scalar(D[:, q, j * P:(j + 1) * P], ident[:, :], tkb[:, q, j:j + 1], None, ALU.mult)
                    last.then_inc(R_["diag"], 1)
                    for j in range(4):
                        ve.tensor_scalar(FV[:, q, j, :], fold, tvb[:, q, j:j + 1], None, ALU.mult)
                    dve.wait_ge(R_["row"], n + 1)
                    for j in range(4):
                        last = ve.tensor_scalar(EQ[:, q, j, :], (T0, T1)[q][:, :], tkb[:, q, j:j + 1], None, ALU.is_equal)
                    last.then_inc(R_["fv"], 1)
                    dve.wait_ge(R_["fv"], n + 1)
                    for j in range(4):
                        ve.tensor_tensor_reduce(junk, EQ[:, q, j, :], before[:, j, :], 1.0, 0.0, ALU.mult, ALU.add,
                                                nfirst[:, q, j:j + 1]).then_inc(R_["cn"], 1)
                        dve.wait_ge(R_["cn"], n * 4 + j + 1)
                    ve.tensor_scalar(nfirst[:, q, :], nfirst[:, q, :], 0.5, float(1 << 20), ALU.is_gt, ALU.mult).then_inc(R_["cnf"], 1)
                    dve.wait_ge(R_["cnf"], n + 1)
                    ve.tensor_tensor(idxs[:, bass.ds(n * 4, 4)], nfirst[:, q, :], tkg_f[:, bass.ds(n * 4, 4)], ALU.add).then_inc(R_["idxs"], 1)
                    dve.wait_ge(s_rows[q], g * 64 + 64)
                    for m in range(2):
                        last = ve.bn_stats(stR[:, q, 2 * m:2 * m + 2, :].rearrange("p n s -> p (n s)"),
                                           R[:, q, 2 * m:2 * m + 2, :].rearrange("p h w -> p w h"))
                    last.then_inc(R_["rbn"], 1)
                    dve.wait_ge(R_["rbn"], n + 1)
                    ve.tensor_scalar(vR[:, q, :], stR[:, q, :, 2], 1.0 / W, EPS_T, ALU.mult, ALU.add).then_inc(R_["rvar"], 1)
                    ve.tensor_tensor(RC[:, q, :, :], R[:, q, :, :], stR[:, q, :, 1].unsqueeze(2).to_broadcast([P, 4, W]), ALU.subtract)
                    dve.wait_ge(R_["rr"], n + 1)
                    ve.tensor_tensor(wvb[:, q, :], tvb[:, q, :], rR[:, q, :], ALU.mult).then_inc(R_["wv"], 1)
                    dve.wait_ge(R_["wv"], n + 1)
                    for j in range(4):
                        last = ve.tensor_scalar(FW[:, q, j, :], fold, wvb[:, q, j:j + 1], None, ALU.mult)
                    last.then_inc(R_["fw"], 1)
            with dve.Fori(0, E // 2) as g:
                for q in range(2):
                    n = g * 2 + q
                    dve.wait_ge(R_["o"], n + 1)
                    ve.tensor_copy(OT[:, :, bass.ds(n, 1)], (T0, T1)[q][:, 0:NB].unsqueeze(2)).then_inc(R_["ot"], 1)
            dve.wait_ge(R_["ot"], E)
            dve.wait_ge(R_["q_done"], NB)
            dve.wait_ge(R_["idxs"], NB)

            def spread(g):
                for q in range(2):
                    n = g * 2 + q
                    wait(dve, s_sc[q], g * 64)
                    ve.tensor_copy(OB[:, q:q + 1, :], OT[:, bass.ds(n, 1), :]).then_inc(R_["ob"], 1)
                    ve.tensor_copy(idxq[:, q, :], idxs[:, bass.ds(n * 4, 4)])
                    ve.tensor_copy(QB[:, q:q + 1, :], Q[:, bass.ds(n, 1), :])
                    dve.wait_ge(R_["obt"], n + 1)
                    ve.tensor_copy(OE[:, q, :], (T0, T1)[q][0:E, 0:P]).then_inc(R_["qb"], 1)

            spread(0)
            with dve.Fori(1, NB // 2) as g:
                spread(g)


_INS = ["x", "L0_conv_wq", "L0_conv_bq", "L0_conv_wk", "L0_conv_bk", "L0_conv_wv", "L0_conv_wo", "L0_conv_gamma",
        "L0_conv_beta", "L0_ffn_gate_w", "L0_ffn_gate_b", "L0_ffn_weight1", "L0_ffn_weight2"]


def kernel(**inputs):
    import numpy as np
    import concourse.bacc as bacc
    from concourse.bass_utils import run_bass_kernel_spmd as run

    nc = bacc.Bacc("TRN2", target_bir_lowering=False, num_devices=1)
    arrays, args = {}, []
    for name in _INS:
        a = np.ascontiguousarray(inputs[name])
        arrays[f"in_{name}"] = a
        args.append(nc.dram_tensor(f"in_{name}", a.shape, F32, kind="ExternalInput").ap())
    shape = inputs["x"].shape
    args.append(nc.dram_tensor("out_dram", shape, F32, kind="ExternalOutput").ap())
    program(nc, *args)
    r = run(nc, [arrays], core_ids=[0])
    return r.results[0]["out_dram"]
```

```python
from contextlib import ExitStack

import concourse.bass as bass
from concourse import mybir

F32 = mybir.dt.float32
U32 = mybir.dt.uint32
ALU = mybir.AluOpType
ACT = mybir.ActivationFunctionType
AX = mybir.AxisListType.X

P = 128
W = 128
TI = 4
NI = P // TI
IC = 4
NK = NI // IC
TC = TI * IC
CW = TC * W
IW = TI * W
XR = 4
NO = 3
HEADS = 8
E = 64
K = 8
EPS_C, EPS_O, EPS_T = 1e-6, 1e-5, 1e-5
SI = 8
NS = NI // SI
SW = SI * TI // 2 * P
HID = 512
HC = HID // P

L_LOAD, L_BNA, L_STA, L_U, L_TRU, L_UT, L_GRAM = 0, 6, 10, 11, 17, 18, 19
S_MUT, S_G, S_A1, S_ATT, S_WP, S_MT = 49, 51, 52, 53, 55, 56
L_MY, L_BNO, L_N, L_GB = 57, 58, 59, 60
L_BNZ, L_STZ, L_STORE = 67, 71, 66
L_TRZ, L_ZT, L_LOG, L_SC, L_TR2, L_LTE = 70, 71, 72, 73, 73, 74
L_MAX, L_MAXI, L_EXP = 82, 86, 87
S_CAND, S_CROSS, S_TOP, S_TEXP, S_FIN = 111, 112, 112, 114, 115

S_GATH, S_POOL, STEP = 70, 72, 1


def program(nc, x, wq, bq, wk, bk, wv, wo, gamma, beta, gate_w, gate_b, w1, w2, out):
    NB = x.shape[0]
    HW = x.shape[2] * x.shape[3]
    SCALE = float(HW) ** -0.5
    LOOP0, LOOPS = 4, (NB - 4) // 2
    LAST = NB + 3
    assert LAST * NI > S_FIN + (NB - 1) * NI and LAST * NI > NB * NI + S_POOL + STEP * (NB - 1)
    x_v = x.rearrange("b c h w -> c b (h w)")
    out_v = out.rearrange("b c h w -> c b (h w)")
    rows_v = out.rearrange("b c h w -> (b c h) w")

    with ExitStack() as ctx:
        def sb(name, shape, dt=F32):
            return ctx.enter_context(nc.sbuf_tensor(name, shape, dt))

        def bank(name):
            return ctx.enter_context(nc.psum_tensor(name, [P, 512], F32))

        def sem(name):
            return ctx.enter_context(nc.semaphore(name))

        U = sb("U", [P, 2, NK, CW])
        xa = sb("xa", [P, XR, CW])
        UT = sb("UT", [P, 2, IW])
        zT = sb("zT", [P, 2, IW])
        Ls = sb("Ls", [P, 2, TI * E])
        LTS = sb("LTS", [P, 2, SW])
        ident = sb("ident", [P, P])
        pick = sb("pick", [P, 2, P])
        gam = sb("gam", [P, W])
        bet = sb("bet", [P, W])
        mask = sb("mask", [P, P])
        nat = sb("nat", [P, 4, P])
        wT = sb("wT", [P, 3, P])
        bqk = sb("bqk", [1, 2, P])
        hbk = sb("hbk", [1, P])
        gwn = LTS[0:E, 0, 0:2 * W].rearrange("p (n w) -> p n w", n=2)
        gws = sb("gws", [E, 2])
        gwT = sb("gwT", [P, E])
        gb2 = sb("gb2", [P, 1])
        stA = sb("stA", [P, 2, TC, 3])
        vA = sb("vA", [P, TC]); sA = sb("sA", [P, TC]); rA = sb("rA", [P, 2, TC])
        MU = sb("MU", [P, 2, P])
        MUT = sb("MUT", [P, 2, P])
        Gs = sb("Gs", [P, P]); A1s = sb("A1s", [P, P]); At = sb("At", [P, P])
        WPs = sb("WPs", [P, P])
        mx = sb("mx", [P, 3])
        MT = sb("MT", [P, 2, P])
        stO = sb("stO", [P, 2, TI, 3])
        vO = sb("vO", [P, 2, TI]); sO = sb("sO", [P, 2, TI]); rO = sb("rO", [P, 2, TI]); mO = sb("mO", [P, 2, TI])
        stZ = sb("stZ", [P, 2, TC, 3])
        vZ = sb("vZ", [P, TC]); sZ = sb("sZ", [P, TC]); rZ = sb("rZ", [P, 2, TC])
        CD = sb("CD", [P, 2, 2 * NS * K + NS])
        CI = sb("CI", [P, 2, NS * K], U32)
        NM = sb("NM", [P, 2, NS])
        ci = sb("ci", [P, 2, NS * K], U32)
        soff = sb("soff", [P, NS * K])
        XV = sb("XV", [P, 2, NS * K]); XT = sb("XT", [P, 2, NS * K]); XS = sb("XS", [P, 2, NS])
        tv = sb("tv", [P, K]); tp = sb("tp", [P, K], U32); tpf = sb("tpf", [P, K]); ng = sb("ng", [P, 1])
        pos = sb("pos", [P, 2 * NS * K])
        hot = sb("hot", [P, K, 2 * NS * K])
        tok8 = sb("tok8", [P, K]); e8 = sb("e8", [P, K]); eL = sb("eL", [P, 2, NS])
        sm = sb("sm", [P, 2 + 2 * NS])
        top8 = sb("top8", [P, K])
        TV = sb("TV", [P, NB * 4])
        TK = sb("TK", [P, NB * 4])

        halves = [U[:, h, :, :].rearrange("p k n -> p (k n)") for h in range(2)]
        used = [0, 0]

        def place(h, *dims, dt=F32, parts=P):
            n = 1
            for d in dims:
                n *= d
            assert used[h] + n <= NK * CW, (h, used)
            v = halves[h][0:parts, used[h]:used[h] + n]
            used[h] += n
            if dt is not F32:
                v = v.bitcast(dt)
            if len(dims) == 2:
                return v.rearrange("p (a b) -> p a b", a=dims[0])
            if len(dims) == 3:
                return v.rearrange("p (a b c) -> p a b c", a=dims[0], b=dims[1])
            return v

        EQ = place(0, NB, 4, P)
        D = place(0, 2, 4, P)
        first = place(0, 2, 4, P)
        before = place(0, P)
        fold = place(0, E)
        FW = place(0, 2, 4, E)
        allone = place(0, P)
        wvb = place(0, 2, 4); nfirst = place(0, 2, 4)
        idx = place(0, NB, 4, dt=U32)
        idxs = place(0, NB, 4, dt=U32)
        rowf = place(0, NB, 4); boff = place(0, NB)
        stR = place(0, 2, 4, 3); vR = place(0, 2, 4); sR = place(0, 2, 4); rR = place(0, 2, 4)
        PT = place(0, E, NB)
        b1s = place(1, HID, parts=E); b2s = place(1, W, parts=E)
        b1T = place(1, HC, E); b2T = place(1, E)
        HB = place(1, 2, HC * NB); HT = place(1, 2, HC * NB)
        OT = place(1, NB, 2, E)
        V = place(1, 2, 4, W)
        CS = 4
        C = place(1, CS, 4, W)
        WR = 8
        wring = place(1, WR, 2 * HID)
        R = xa[:, :, :].rearrange("p a (b j w) -> p (a b) j w", j=4, w=W)
        w1v = w1.rearrange("e d h -> d e h")
        w2v = w2[:, 0:HID, :].rearrange("e (c p) o -> p e c o", p=P)

        T0, T1, G, LM, LT = (bank(n) for n in ("T0", "T1", "G", "LM", "LT"))
        O = [bank(f"O{i}") for i in range(NO)]
        L, MB = LM[:, 0:TI * E], LM[:, TI * E:512]

        s_const = sem("s_const"); s_iota = sem("s_iota"); s_setup = sem("s_setup"); s_wtp = sem("s_wtp"); s_wtc = sem("s_wtc")
        s_x = [sem(f"s_x{i}") for i in range(XR)]
        s_acc = [sem(f"s_acc{i}") for i in range(2 * NK)]
        s_store = [sem(f"s_store{i}") for i in range(2 * NK)]
        s_setup_dve = sem("s_setup_dve")
        names = ("a_bn a_var a_ln a_rstd a_mu u_ready tru ut_ready gram mut muts g g_copied a1 a1s att att_s "
                 "nmx pexp prs p_ready wp wps mt mt_ready my o_bn o_var o_ln o_r o_rs n_done pool_g gb "
                 "z_bn z_var z_ln z_r trz zt_ready lg l_scaled tr2 lt_done seg_v seg_i seg_nm seg_exp "
                 "tick c1 cand cross crossed t1 t2 texp fin").split()
        S = {n: sem("s_" + n) for n in names}
        s_tail = sem("s_tail"); s_prep = sem("s_prep"); s_bias = sem("s_bias")
        s_rows = [sem(f"s_rows{i}") for i in range(4)]; s_sc = [sem(f"s_sc{i}") for i in range(CS)]
        s_w = [sem(f"s_w{i}") for i in range(WR)]
        tnames = ("rowf idx diag row eq fst nf idxs rbn rvar rln rr wv cen fw pmm p_done "
                  "bt btc h hb ht o ot xt v cmm c").split()
        R_ = {n: sem("r_" + n) for n in tnames}

        def val(b):
            c, it = b
            return c if it is None else it * 2 + c

        def cnt(b, per, extra):
            c, it = b
            base = c * per + extra
            return base if it is None else it * (2 * per) + base

        def item(b, t, lag, per=1):
            c, it = b
            off, i = divmod(t - lag, NI)
            if it is None and not 0 <= c + off < NB:
                return None
            return ((c + off, it), i // per) if i % per == 0 else None

        def late(b, t, start):
            c, it = b
            n, rest = divmod((c - NB) * NI + t - start, STEP)
            return n if it is None and rest == 0 and 0 <= n < NB else None

        def wait(eng, s, value):
            if not (isinstance(value, int) and value <= 0):
                eng.wait_ge(s, value)

        def dma_uses(b, extra=0):
            c, it = b
            base = 16 * (c // 2 + 1 + extra)
            return base if it is None else it * 16 + base

        def bodies(eng, body):
            for c in range(LOOP0):
                body((c, None))
            with eng.Fori(0, LOOPS) as it:
                body((LOOP0, it))
                body((LOOP0 + 1, it))
            for c in range(NB, LAST):
                body((c, None))

        def chunk(b, k):
            return U[:, b[0] % 2, k, :]

        def utile(b, i, j):
            o = (i % IC) * IW + j * W
            return U[:, b[0] % 2, i // IC, o:o + W]

        def pair(ap, n):
            return ap[:, 2 * n * W:(2 * n + 2) * W].rearrange("p (h w) -> p w h", h=2)

        NCONST = 16 * 11
        block = ctx.enter_context(nc.Block())

        @block.sync
        def _(sp):
            for i, w in enumerate((wq, wk, wv, wo)):
                sp.dma_start(nat[:, i, :], w).then_inc(s_const, 16)
            sp.dma_start(bqk[:, 0, :], bq.rearrange("(a n) -> a n", a=1)).then_inc(s_const, 16)
            sp.dma_start(bqk[:, 1, :], bk.rearrange("(a n) -> a n", a=1)).then_inc(s_const, 16)
            sp.dma_start(gam[:, :], gamma.rearrange("(a n) -> a n", a=1).to_broadcast([P, W])).then_inc(s_const, 16)
            sp.dma_start(bet[:, :], beta.rearrange("(a n) -> a n", a=1).to_broadcast([P, W])).then_inc(s_const, 16)
            sp.dma_start(gwn[:, 0, :], gate_w).then_inc(s_const, 16)
            for g in range(2):
                sp.dma_start(gb2[g * E:(g + 1) * E, :], gate_b.rearrange("(e a) -> e a", a=1)).then_inc(s_const, 16)

            def body(b):
                for t in range(NI):
                    if r := item(b, t, L_LOAD, IC):
                        a, k = r
                        wait(sp, S["u_ready"], cnt(a, NK, k - XR + 1))
                        bv = val(a)
                        sp.dma_start(xa[:, k % XR:k % XR + 1, :],
                                     x_v[:, bass.ds(bv, 1), k * CW:(k + 1) * CW]).then_inc(s_x[k % XR], 16)
                    if r := item(b, t, L_STORE, IC):
                        a, k = r
                        n = a[0] % 2 * NK + k
                        wait(sp, s_acc[n], dma_uses(a))
                        bv = val(a)
                        sp.dma_start(out_v[:, bass.ds(bv, 1), k * CW:(k + 1) * CW],
                                     U[:, a[0] % 2, k:k + 1, :]).then_inc(s_store[n], 16)

            bodies(sp, body)
            sp.wait_ge(S["trz"], NB * NI)
            for n in range(2 * NK):
                sp.wait_ge(s_store[n], 16 * (NB // 2))
            sp.sem_inc(s_tail, 1)
            sp.dma_start(b1s, w1[:, W, :]).then_inc(s_bias, 16)
            sp.dma_start(b2s, w2[:, HID, :]).then_inc(s_bias, 16)

            def weights(e, n, s, first):
                if not first:
                    sp.wait_ge(R_["o"], n - WR + 1)
                sp.dma_start(wring[:, s:s + 1, 0:HID], w1v[0:W, bass.ds(e, 1), :]).then_inc(s_w[s], 16)
                sp.dma_start(wring[:, s, HID:2 * HID].rearrange("p (a c o) -> p a c o", a=1, c=HC),
                             w2v[:, bass.ds(e, 1), :, :]).then_inc(s_w[s], 16)

            for s in range(WR):
                weights(s, s, s, True)
            with sp.Fori(1, E // WR) as g:
                for s in range(WR):
                    weights(g * WR + s, g * WR + s, s, False)
            for q in range(CS):
                sp.wait_ge(s_sc[q], 64 * (NB // CS))

        @block.gpsimd
        def _(pool):
            gp = nc.gpsimd
            gp.memset(ident[:, :], 0.0).then_inc(s_iota, 1)
            gp.memset(mask[:, :], 0.0).then_inc(s_iota, 1)
            gp.memset(pick[:, :, :], 0.0).then_inc(s_iota, 1)
            pool.wait_ge(s_iota, 3)
            gp.affine_select(out=ident[:, :], in_=ident[:, :], compare_op=ALU.not_equal, fill=1.0, base=0,
                             pattern=[[-1, P]], channel_multiplier=1).then_inc(s_iota, 1)
            hd = P // HEADS
            mv = mask[:, :].rearrange("p (h d) -> p h d", d=hd)
            gp.affine_select(out=mv, in_=mv, compare_op=ALU.is_ge, fill=-1e30, base=0,
                             pattern=[[-hd, HEADS], [0, hd]], channel_multiplier=1).then_inc(s_iota, 1)
            for g in range(2):
                pv = pick[:, g, :].rearrange("p (r e) -> p r e", r=2)
                gp.affine_select(out=pv, in_=pv, compare_op=ALU.not_equal, fill=1.0, base=-g * E,
                                 pattern=[[0, 2], [-1, E]], channel_multiplier=1).then_inc(s_iota, 1)
            pool.wait_ge(s_iota, 7)
            gp.affine_select(out=mv, in_=mv, compare_op=ALU.is_ge, fill=-1e30, base=hd - 1,
                             pattern=[[hd, HEADS], [0, hd]], channel_multiplier=-1).then_inc(s_iota, 1)
            for g in range(2):
                pool.wait_ge(s_iota, 8 + g)
                gp.iota(soff[g * E:(g + 1) * E, :].rearrange("p (s k) -> p s k", k=K),
                        pattern=[[2 * SI * TI // 2, NS], [0, K]], base=g, channel_multiplier=0,
                        allow_small_or_imprecise_dtypes=True).then_inc(s_iota, 1)
            pool.wait_ge(s_iota, 10)
            gp.iota(pos[:, :], pattern=[[1, 2 * NS * K]], base=0, channel_multiplier=0,
                    allow_small_or_imprecise_dtypes=True).then_inc(s_iota, 1)
            pool.wait_ge(s_const, NCONST)

            gam_b = gam[:, :].unsqueeze(1).to_broadcast([P, 2 * TI, W])
            bet_b = bet[:, :].unsqueeze(1).to_broadcast([P, 2 * TI, W])

            def gather(n):
                if n == 0:
                    pool.wait_ge(s_tail, 1)
                    gp.memset(before, 1.0).then_inc(s_prep, 1)
                    gp.memset(allone, 1.0).then_inc(s_prep, 1)
                    gp.iota(boff, pattern=[[HW, NB]], base=0, channel_multiplier=0,
                            allow_small_or_imprecise_dtypes=True).then_inc(s_prep, 1)
                    pool.wait_ge(s_prep, 3)
                    gp.affine_select(out=before, in_=before, compare_op=ALU.is_gt, fill=0.0,
                                     base=0, pattern=[[-1, P]], channel_multiplier=1).then_inc(s_prep, 1)
                pool.wait_ge(R_["idx"], n + 1)
                wait(pool, R_["rbn"], n - 3)
                for j in range(4):
                    gp.indirect_dma_start(out=R[:, n, j, :], out_offset=None, in_=rows_v,
                                          in_offset=bass.IndirectOffsetOnAxis(ap=idx[:, n, j:j + 1], axis=0),
                                          ).then_inc(s_rows[n % 4], 16)

            def body(b):
                for t in range(NI):
                    if r := item(b, t, L_U, IC):
                        a, k = r
                        pool.wait_ge(S["a_rstd"], cnt(a, NK, k + 1))
                        wait(pool, S["trz"], cnt(a, NI, IC * k + IC - 2 * NI))
                        wait(pool, s_store[a[0] % 2 * NK + k], dma_uses(a, -1))
                        gp.tensor_tensor(chunk(a, k).rearrange("p (h w) -> p h w", w=W),
                                         xa[:, k % XR, :].rearrange("p (h w) -> p h w", w=W),
                                         rA[:, k % 2, :].unsqueeze(2).to_broadcast([P, TC, W]),
                                         ALU.mult).then_inc(S["u_ready"], 1)
                    if r := item(b, t, L_GB):
                        a, i = r
                        if i % 2 == 1:
                            p = i // 2
                            pool.wait_ge(S["n_done"], cnt(a, NI, i + 1))
                            o = p % 2 * 2 * IW
                            v = chunk(a, i // IC)[:, o:o + 2 * IW].rearrange("p (h w) -> p h w", w=W)
                            gp.tensor_tensor(v, v, gam_b, ALU.mult).then_inc(S["pool_g"], 1)
                            pool.wait_ge(S["pool_g"], cnt(a, NI // 2, p + 1))
                            gp.tensor_tensor(v, v, bet_b, ALU.add).then_inc(S["gb"], 1)
                            if p % 2 == 1:
                                k = i // IC
                                pool.wait_ge(S["gb"], cnt(a, NI // 2, p + 1))
                                bv = val(a)
                                gp.dma_start(U[:, a[0] % 2, k:k + 1, :],
                                             x_v[:, bass.ds(bv, 1), k * CW:(k + 1) * CW],
                                             accum_op=ALU.add).then_inc(s_acc[a[0] % 2 * NK + k], 16)
                    if (n := late(b, t, S_GATH)) is not None:
                        gather(n)

            bodies(pool, body)
            for g in range(0, NB, CS):
                for j in range(4):
                    for n in range(g, g + CS):
                        q = n % CS
                        if j == 0:
                            pool.wait_ge(R_["c"], n + 1)
                        else:
                            pool.wait_ge(s_sc[q], (n // CS) * 64 + j * 16)
                        gp.indirect_dma_start(out=rows_v,
                                              out_offset=bass.IndirectOffsetOnAxis(ap=idxs[:, n, j:j + 1], axis=0),
                                              in_=C[:, q, j, :], in_offset=None,
                                              bounds_check=NB * P * P - 1, oob_is_err=False,
                                              compute_op=ALU.add).then_inc(s_sc[q], 16)

        @block.scalar
        def _(act):
            sc = nc.scalar
            sc.preload_act_table_set("natural_log_exp_and_others")

            def body(b):
                for t in range(NI):
                    if r := item(b, t, L_UT):
                        a, i = r
                        act.wait_ge(S["tru"], cnt(a, NI, i + 1))
                        wait(act, S["gram"], cnt(a, NI, i - 1))
                        sc.activation(UT[:, i % 2, :], T0[:, :], ACT.Copy).then_inc(S["ut_ready"], 1)
                    if r := item(b, t, L_ZT):
                        a, i = r
                        act.wait_ge(S["trz"], cnt(a, NI, i + 1))
                        wait(act, S["lg"], cnt(a, NI, i - 1))
                        sc.activation(zT[:, i % 2, :], T1[:, :], ACT.Copy).then_inc(S["zt_ready"], 1)
                    if r := item(b, t, L_BNO):
                        a, i = r
                        act.wait_ge(S["o_var"], cnt(a, NI, i + 1))
                        sc.activation(sO[:, i % 2, :], vO[:, i % 2, :], ACT.Ln).then_inc(S["o_ln"], 1)
                        act.wait_ge(S["o_ln"], cnt(a, NI, i + 1))
                        sc.activation(rO[:, i % 2, :], sO[:, i % 2, :], ACT.Exp, scale=-0.5).then_inc(S["o_r"], 1)
                    if r := item(b, t, L_LTE):
                        a, i = r
                        act.wait_ge(S["tr2"], cnt(a, NI, i + 1))
                        s = i // SI
                        if i % SI == 0:
                            wait(act, S["seg_exp"], cnt(a, NS, s - 1))
                        o = i % SI * TI * E
                        sc.activation(LTS[:, s % 2, o:o + TI * E], LT[:, 0:TI * E], ACT.Identity,
                                      bias=gb2[:, 0:1]).then_inc(S["lt_done"], 1)
                    if r := item(b, t, L_N):
                        a, i = r
                        act.wait_ge(S["o_rs"], cnt(a, NI, i + 1))
                        for j in range(TI):
                            last = sc.activation(utile(a, i, j), O[i % NO][:, j * W:(j + 1) * W], ACT.Identity,
                                                 scale=rO[:, i % 2, j:j + 1], bias=mO[:, i % 2, j:j + 1])
                        last.then_inc(S["n_done"], 1)
                    if r := item(b, t, L_STA, IC):
                        a, k = r
                        act.wait_ge(S["a_var"], cnt(a, NK, k + 1))
                        sc.activation(sA[:, :], vA[:, :], ACT.Ln).then_inc(S["a_ln"], 1)
                        act.wait_ge(S["a_ln"], cnt(a, NK, k + 1))
                        sc.activation(rA[:, k % 2, :], sA[:, :], ACT.Exp, scale=-0.5).then_inc(S["a_rstd"], 1)
                    if r := item(b, t, L_STZ, IC):
                        a, k = r
                        act.wait_ge(S["z_var"], cnt(a, NK, k + 1))
                        sc.activation(sZ[:, :], vZ[:, :], ACT.Ln).then_inc(S["z_ln"], 1)
                        act.wait_ge(S["z_ln"], cnt(a, NK, k + 1))
                        sc.activation(rZ[:, k % 2, :], sZ[:, :], ACT.Exp, scale=-0.5).then_inc(S["z_r"], 1)
                    if r := item(b, t, L_EXP, SI):
                        a, s = r
                        act.wait_ge(S["seg_nm"], cnt(a, NS, s + 1))
                        sc.activation(LTS[:, s % 2, :], LTS[:, s % 2, :], ACT.Exp, bias=NM[:, a[0] % 2, s:s + 1],
                                      accum_out=CD[:, a[0] % 2, 2 * NS * K + s:2 * NS * K + s + 1]).then_inc(S["seg_exp"], 1)
                    if (r := item(b, t, S_ATT, NI)):
                        a, _ = r
                        act.wait_ge(S["nmx"], cnt(a, 1, 1))
                        sc.activation(At[:, :], At[:, :], ACT.Exp, bias=mx[:, 0:1],
                                      accum_out=mx[:, 1:2]).then_inc(S["pexp"], 1)
                    if (r := item(b, t, S_TEXP, NI)):
                        a, _ = r
                        act.wait_ge(S["t1"], cnt(a, 4, 4))
                        sc.activation(e8[:, :], tv[:, :], ACT.Exp, bias=ng[:, 0:1])
                        sc.activation(eL[:, :, :], XV[:, :, 0:NS * K:K], ACT.Exp, bias=ng[:, 0:1]).then_inc(S["texp"], 1)
                    if (n := late(b, t, S_POOL)) is not None:
                        act.wait_ge(R_["rvar"], n + 1)
                        sc.activation(sR[:, n % 2, :], vR[:, n % 2, :], ACT.Ln).then_inc(R_["rln"], 1)
                        act.wait_ge(R_["rln"], n + 1)
                        sc.activation(rR[:, n % 2, :], sR[:, n % 2, :], ACT.Exp, scale=-0.5).then_inc(R_["rr"], 1)
                    if (n := late(b, t, S_POOL + 1)) is not None:
                        act.wait_ge(R_["pmm"], n + 1)
                        sc.activation(PT[:, :, n:n + 1], O[n % 2][:, 0:E].unsqueeze(2), ACT.Copy).then_inc(R_["p_done"], 1)

            bodies(act, body)

            with act.Fori(0, E // 2) as g:
                for q in range(2):
                    n = g * 2 + q
                    act.wait_ge(R_["hb"], n + 1)
                    sc.activation(HT[:, q, :], HB[:, q, :], ACT.Gelu).then_inc(R_["ht"], 1)
            for n in range(NB):
                act.wait_ge(R_["cmm"], n + 1)
                wait(act, s_sc[n % CS], n // CS * 64)
                sc.activation(C[:, n % CS, :, :].rearrange("p j w -> p (j w)"), O[n % 2][:, :], ACT.Copy).then_inc(R_["c"], 1)

        @block.tensor
        def _(pe):
            te = nc.tensor
            pe.wait_ge(s_iota, 7)
            pe.wait_ge(s_const, NCONST)
            for n, i in enumerate((0, 1, 3)):
                last = te.transpose(T0[:, n * P:(n + 1) * P], nat[:, i, :], ident[:, :])
            last.then_inc(s_wtp, 1)
            pe.wait_ge(s_setup, 1)
            te.transpose(L[:, 0:E], gwn[:, 1, :], ident[0:E, 0:E]).then_inc(s_wtp, 1)
            pe.wait_ge(s_wtc, 2)

            def product(a, i):
                if i == 0:
                    pe.wait_ge(S["mt_ready"], cnt(a, 1, 1))
                wait(pe, S["n_done"], cnt(a, NI, i - NO + 1 if i >= NO else i - 1))
                o = i % IC * IW
                te.matmul(O[i % NO][:, :], MT[:, a[0] % 2, :], chunk(a, i // IC)[:, o:o + IW],
                          start=True, stop=True).then_inc(S["my"], 1)

            def body(b):
                for t in range(NI):
                    if (r := item(b, t, L_MY)) and r[1] >= 2:
                        product(*r)
                    if r := item(b, t, L_GRAM):
                        a, i = r
                        pe.wait_ge(S["ut_ready"], cnt(a, NI, i + 1))
                        if i == 0:
                            wait(pe, S["g_copied"], cnt(a, 1, 0))
                        for j in range(TI):
                            v = UT[:, i % 2, j * W:(j + 1) * W]
                            last = te.matmul(G[:, 0:P], v, v, start=(i == 0 and j == 0), stop=False)
                        last.then_inc(S["gram"], 1)
                        if i == NI - 1:
                            pe.wait_ge(S["muts"], cnt(a, 1, 1))
                            te.matmul(G[:, 0:P], MUT[:, 1, :], MUT[:, 0, :], start=False, stop=True).then_inc(S["g"], 1)
                    if any(item(b, t, stage, NI) for stage in (S_CROSS, S_MUT, S_A1, S_ATT, S_WP, S_MT)):
                        if r := item(b, t - 1, L_LOG):
                            pe.wait_ge(S["l_scaled"], cnt(r[0], NI, r[1] + 1))
                    if (r := item(b, t, S_CROSS, NI)):
                        a, _ = r
                        pe.wait_ge(S["cand"], cnt(a, 1, 1))
                        pe.wait_ge(S["seg_exp"], cnt(a, NS, NS))
                        c, it = a
                        pe.wait_ge(S["mt_ready"], cnt(a, 1, 2 if it is not None else min(2, NB - c)))
                        n = 2 * NS * K + NS
                        for g in range(2):
                            last = te.matmul(MB[:, g * n:(g + 1) * n], pick[:, g, :], CD[:, a[0] % 2, :], start=True, stop=True)
                        last.then_inc(S["cross"], 1)
                    if (r := item(b, t, S_MUT, NI)):
                        a, _ = r
                        pe.wait_ge(S["a_mu"], cnt(a, NK, NK))
                        wait(pe, S["crossed"], cnt(a, 1, -1))
                        wait(pe, S["mt_ready"], cnt(a, 1, 0))
                        te.transpose(MB[:, 0:P], MU[:, a[0] % 2, :], ident[:, :]).then_inc(S["mut"], 1)
                    if (r := item(b, t, S_A1, NI)):
                        a, _ = r
                        pe.wait_ge(S["g_copied"], cnt(a, 1, 1))
                        te.matmul(MB[:, 0:P], Gs[:, :], wT[:, 1, :], start=True, stop=True).then_inc(S["a1"], 1)
                    if (r := item(b, t, S_ATT, NI)):
                        a, _ = r
                        pe.wait_ge(S["a1s"], cnt(a, 1, 1))
                        te.matmul(MB[:, 0:P], wT[:, 0, :], A1s[:, :], start=True, stop=False)
                        te.matmul(MB[:, 0:P], bqk[:, 0, :], hbk[:, :], start=False, stop=True).then_inc(S["att"], 1)
                    if (r := item(b, t, S_WP, NI)):
                        a, _ = r
                        pe.wait_ge(S["p_ready"], cnt(a, 1, 1))
                        te.matmul(MB[:, 0:P], At[:, :], wT[:, 2, :], start=True, stop=True).then_inc(S["wp"], 1)
                    if (r := item(b, t, S_MT, NI)):
                        a, _ = r
                        pe.wait_ge(S["wps"], cnt(a, 1, 1))
                        te.matmul(MB[:, 0:P], nat[:, 2, :], WPs[:, :], start=True, stop=True).then_inc(S["mt"], 1)
                    if r := item(b, t, L_TRU):
                        a, i = r
                        if i % IC == 0:
                            pe.wait_ge(S["u_ready"], cnt(a, NK, i // IC + 1))
                        wait(pe, S["ut_ready"], cnt(a, NI, i))
                        for j in range(TI):
                            last = te.transpose(T0[:, j * W:(j + 1) * W], utile(a, i, j), ident[:, :])
                        last.then_inc(S["tru"], 1)
                    if r := item(b, t, L_TR2):
                        a, i = r
                        pe.wait_ge(S["l_scaled"], cnt(a, NI, i + 1))
                        wait(pe, S["lt_done"], cnt(a, NI, i))
                        for j in range(TI // 2):
                            last = te.transpose(LT[:, j * P:(j + 1) * P], Ls[:, i % 2, j * P:(j + 1) * P], ident[:, :])
                        last.then_inc(S["tr2"], 1)
                    if r := item(b, t, L_LOG):
                        a, i = r
                        pe.wait_ge(S["zt_ready"], cnt(a, NI, i + 1))
                        wait(pe, S["l_scaled"], cnt(a, NI, i))
                        for stage, read in ((S_CROSS, "crossed"), (S_MUT, "muts"), (S_A1, "a1s"), (S_ATT, "att_s"),
                                            (S_WP, "wps"), (S_MT, "mt_ready")):
                            if m := item(b, t, stage, NI):
                                pe.wait_ge(S[read], cnt(m[0], 1, 1))
                        for j in range(TI):
                            last = te.matmul(L[:, j * E:(j + 1) * E], zT[:, i % 2, j * W:(j + 1) * W], gwT[:, :],
                                             start=True, stop=True)
                        last.then_inc(S["lg"], 1)
                    if r := item(b, t, L_TRZ):
                        a, i = r
                        if i % IC == 0:
                            pe.wait_ge(s_acc[a[0] % 2 * NK + i // IC], dma_uses(a))
                        wait(pe, S["zt_ready"], cnt(a, NI, i))
                        for j in range(TI):
                            last = te.transpose(T1[:, j * W:(j + 1) * W], utile(a, i, j), ident[:, :])
                        last.then_inc(S["trz"], 1)
                    if (r := item(b, t, L_MY)) and r[1] < 2:
                        product(*r)
                    if (n := late(b, t, S_POOL)) is not None:
                        pe.wait_ge(R_["diag"], n + 1)
                        wait(pe, R_["eq"], n - 1)
                        te.matmul((G, O[2])[n % 2][:, :], allone, D[:, n % 2, :, :].rearrange("p j w -> p (j w)"),
                                  start=True, stop=True).then_inc(R_["row"], 1)
                    if (n := late(b, t, S_POOL + 1)) is not None:
                        pe.wait_ge(R_["fw"], n + 1)
                        wait(pe, R_["p_done"], n - 1)
                        for j in range(4):
                            last = te.matmul(O[n % 2][:, 0:E], R[:, n, j, :], FW[:, n % 2, j, :], start=(j == 0), stop=(j == 3))
                        last.then_inc(R_["pmm"], 1)

            bodies(pe, body)
            pe.wait_ge(s_bias, 32)
            pe.wait_ge(R_["eq"], NB)
            for c in range(HC):
                te.transpose(G[:, c * E:(c + 1) * E], b1s[:, c * P:(c + 1) * P], ident[0:E, 0:E])
            te.transpose(G[:, HC * E:(HC + 1) * E], b2s, ident[0:E, 0:E]).then_inc(R_["bt"], 1)
            pe.wait_ge(R_["btc"], 1)
            pe.wait_ge(R_["p_done"], NB)

            def hidden(n, s, uses):
                pe.wait_ge(s_w[s], uses)
                for c in range(HC):
                    last = te.matmul((G, O[2])[s % 2][:, c * NB:(c + 1) * NB], wring[:, s, c * P:(c + 1) * P],
                                     PT[:, bass.ds(n, 1), :], start=True, stop=True)
                last.then_inc(R_["h"], 1)

            def output(n, s):
                pe.wait_ge(R_["ht"], n + 1)
                wait(pe, R_["ot"], n - 1)
                for c in range(HC):
                    last = te.matmul((T0, T1)[s % 2][:, 0:NB], wring[:, s, HID + c * P:HID + (c + 1) * P],
                                     HT[:, s % 2, c * NB:(c + 1) * NB], start=(c == 0), stop=(c == HC - 1))
                last.then_inc(R_["o"], 1)

            hidden(0, 0, 32)
            for s in range(1, WR):
                hidden(s, s, 32)
                output(s - 1, s - 1)
            with pe.Fori(1, E // WR) as g:
                for s in range(WR):
                    hidden(g * WR + s, s, g * 32 + 32)
                    output(g * WR + s - 1, (s - 1) % WR)
            output(E - 1, WR - 1)
            pe.wait_ge(R_["ot"], E)

            def turn(n):
                te.transpose((T0, T1)[n % 2][:, 0:P], OT[:, n, :, :].rearrange("p g e -> p (g e)"), ident[:, :]).then_inc(R_["xt"], 1)

            turn(0)
            for n in range(NB):
                if n + 1 < NB:
                    wait(pe, R_["v"], n)
                    turn(n + 1)
                pe.wait_ge(R_["v"], n + 1)
                wait(pe, R_["c"], n - 1)
                for j in range(4):
                    last = te.matmul(O[n % 2][:, j * P:(j + 1) * P], EQ[:, n, j, :], V[:, n % 2, j, :], start=True, stop=True)
                last.then_inc(R_["cmm"], 1)

        @block.vector
        def _(dve):
            ve = nc.vector
            dve.wait_ge(s_const, NCONST)
            chain = [0]

            def link(ins):
                chain[0] += 1
                ins.then_inc(s_setup_dve, 1)
                dve.wait_ge(s_setup_dve, chain[0])

            link(ve.tensor_scalar(hbk[:, :], bqk[:, 1, :], float(HW), None, ALU.mult))
            link(ve.tensor_reduce(gws[:, 0:1], gwn[:, 0, :], AX, ALU.add))
            link(ve.tensor_scalar(gws[:, 1:2], gws[:, 0:1], 1.0 / W, None, ALU.mult))
            ve.tensor_scalar(gwn[:, 1, :], gwn[:, 0, :], gws[:, 1:2], None, ALU.subtract).then_inc(s_setup, 1)
            dve.wait_ge(s_wtp, 1)
            ve.tensor_copy(wT[:, :, :], T0[:, 0:3 * P].rearrange("p (n f) -> p n f", n=3)).then_inc(s_wtc, 1)
            dve.wait_ge(s_wtp, 2)
            ve.tensor_copy(gwT[:, :], L[:, 0:E]).then_inc(s_wtc, 1)
            dve.wait_ge(s_iota, 11)

            def body(b):
                for t in range(NI):
                    if (r := item(b, t, S_G, NI)):
                        a, _ = r
                        dve.wait_ge(S["g"], cnt(a, 1, 1))
                        ve.tensor_copy(Gs[:, :], G[:, 0:P]).then_inc(S["g_copied"], 1)
                    if r := item(b, t, L_BNO):
                        a, i = r
                        dve.wait_ge(S["my"], cnt(a, NI, i + 1))
                        for n in range(TI // 2):
                            last = ve.bn_stats(stO[:, i % 2, 2 * n:2 * n + 2, :].rearrange("p n s -> p (n s)"), pair(O[i % NO], n))
                        last.then_inc(S["o_bn"], 1)
                        dve.wait_ge(S["o_bn"], cnt(a, NI, i + 1))
                        ve.tensor_scalar(vO[:, i % 2, :], stO[:, i % 2, :, 2], 1.0 / W, EPS_O, ALU.mult, ALU.add).then_inc(S["o_var"], 1)
                    if r := item(b, t, L_SC):
                        a, i = r
                        dve.wait_ge(S["lg"], cnt(a, NI, i + 1))
                        wait(dve, S["tr2"], cnt(a, NI, i - 1))
                        ve.tensor_tensor(Ls[:, i % 2, :].rearrange("p (h e) -> p h e", e=E),
                                         L[:, 0:TI * E].rearrange("p (h e) -> p h e", e=E),
                                         rZ[:, i // IC % 2, i % IC * TI:(i % IC + 1) * TI].unsqueeze(2).to_broadcast([P, TI, E]),
                                         ALU.mult).then_inc(S["l_scaled"], 1)
                    if (r := item(b, t, S_TOP, NI)):
                        a, _ = r
                        dve.wait_ge(S["cross"], cnt(a, 1, 1))
                        n = 2 * NS * K + NS
                        mv = MB[:, 0:2 * n].rearrange("p (g n) -> p g n", g=2)
                        ve.tensor_copy(XV[:, :, :], mv[:, :, 0:NS * K])
                        ve.tensor_copy(XT[:, :, :], mv[:, :, NS * K:2 * NS * K])
                        ve.tensor_copy(XS[:, :, :], mv[:, :, 2 * NS * K:n]).then_inc(S["crossed"], 1)
                        dve.wait_ge(S["crossed"], cnt(a, 1, 1))
                        xv = XV[:, :, :].rearrange("p g n -> p (g n)")
                        dve.sem_inc(S["tick"], 1)
                        ve.max(tv[:, :], xv).then_inc(S["t1"], 1)
                        dve.wait_ge(S["t1"], cnt(a, 4, 1))
                        ve.tensor_scalar(ng[:, :], tv[:, 0:1], -1.0, None, ALU.mult)
                        dve.sem_inc(S["tick"], 1)
                        ve.max_index(tp[:, :], tv[:, :], xv).then_inc(S["t1"], 1)
                        dve.wait_ge(S["t1"], cnt(a, 4, 2))
                        ve.tensor_copy(tpf[:, :], tp[:, :]).then_inc(S["t1"], 1)
                        dve.wait_ge(S["t1"], cnt(a, 4, 3))
                        M = 2 * NS * K
                        ve.tensor_tensor(hot[:, :, :], pos[:, :].unsqueeze(1).to_broadcast([P, K, M]),
                                         tpf[:, :].unsqueeze(2).to_broadcast([P, K, M]), ALU.is_equal).then_inc(S["t1"], 1)
                    if (r := item(b, t, S_MUT, NI)):
                        a, _ = r
                        dve.wait_ge(S["mut"], cnt(a, 1, 1))
                        ve.tensor_copy(MUT[:, 0, :], MB[:, 0:P])
                        ve.tensor_scalar(MUT[:, 1, :], MB[:, 0:P], -float(W), None, ALU.mult).then_inc(S["muts"], 1)
                    if (r := item(b, t, S_A1, NI)):
                        a, _ = r
                        dve.wait_ge(S["a1"], cnt(a, 1, 1))
                        ve.tensor_copy(A1s[:, :], MB[:, 0:P]).then_inc(S["a1s"], 1)
                    if (r := item(b, t, S_ATT, NI)):
                        a, _ = r
                        dve.wait_ge(S["att"], cnt(a, 1, 1))
                        ve.scalar_tensor_tensor(At[:, :], MB[:, 0:P], SCALE, mask[:, :], ALU.mult, ALU.add).then_inc(S["att_s"], 1)
                        dve.wait_ge(S["att_s"], cnt(a, 1, 1))
                        ve.tensor_reduce(mx[:, 0:1], At[:, :], AX, ALU.max, negate=True).then_inc(S["nmx"], 1)
                    if (r := item(b, t, S_ATT + 1, NI)):
                        a, _ = r
                        dve.wait_ge(S["pexp"], cnt(a, 1, 1))
                        ve.reciprocal(mx[:, 2:3], mx[:, 1:2]).then_inc(S["prs"], 1)
                        dve.wait_ge(S["prs"], cnt(a, 1, 1))
                        ve.tensor_scalar(At[:, :], At[:, :], mx[:, 2:3], None, ALU.mult).then_inc(S["p_ready"], 1)
                    if (r := item(b, t, S_WP, NI)):
                        a, _ = r
                        dve.wait_ge(S["wp"], cnt(a, 1, 1))
                        ve.tensor_copy(WPs[:, :], MB[:, 0:P]).then_inc(S["wps"], 1)
                    if (r := item(b, t, S_MT, NI)):
                        a, _ = r
                        dve.wait_ge(S["mt"], cnt(a, 1, 1))
                        ve.tensor_copy(MT[:, a[0] % 2, :], MB[:, 0:P]).then_inc(S["mt_ready"], 1)
                    if r := item(b, t, L_STA + 1, IC):
                        a, k = r
                        dve.wait_ge(S["a_rstd"], cnt(a, NK, k + 1))
                        ve.tensor_tensor(MU[:, a[0] % 2, k * TC:(k + 1) * TC], stA[:, k % 2, :, 1], rA[:, k % 2, :], ALU.mult).then_inc(S["a_mu"], 1)
                    if r := item(b, t, L_STZ + 1, IC):
                        a, k = r
                        dve.wait_ge(S["z_r"], cnt(a, NK, k + 1))
                    if r := item(b, t, L_BNA):
                        a, i = r
                        k = i // IC
                        if i % IC == 0:
                            c, it = a
                            base = 16 * (2 * c + k // XR + 1)
                            dve.wait_ge(s_x[k % XR], base if it is None else it * 64 + base)
                            wait(dve, S["a_mu"], cnt(a, NK, k - 1))
                        for n in range(TI // 2):
                            j = i % IC * TI + 2 * n
                            last = ve.bn_stats(stA[:, k % 2, j:j + 2, :].rearrange("p n s -> p (n s)"), pair(xa[:, k % XR, :], j // 2))
                        last.then_inc(S["a_bn"], 1)
                    if r := item(b, t, L_STA, IC):
                        a, k = r
                        dve.wait_ge(S["a_bn"], cnt(a, NI, IC * k + IC))
                        wait(dve, S["u_ready"], cnt(a, NK, k - 1))
                        ve.tensor_scalar(vA[:, :], stA[:, k % 2, :, 2], 1.0 / W, EPS_C, ALU.mult, ALU.add).then_inc(S["a_var"], 1)
                    if r := item(b, t, L_BNO):
                        a, i = r
                        dve.wait_ge(S["o_r"], cnt(a, NI, i + 1))
                        ve.scalar_tensor_tensor(mO[:, i % 2, :], stO[:, i % 2, :, 1], -1.0, rO[:, i % 2, :], ALU.mult, ALU.mult).then_inc(S["o_rs"], 1)
                    if r := item(b, t, L_BNZ):
                        a, i = r
                        k = i // IC
                        if i % IC == 0:
                            dve.wait_ge(s_acc[a[0] % 2 * NK + k], dma_uses(a))
                        for n in range(TI // 2):
                            j = i % IC * TI + 2 * n
                            last = ve.bn_stats(stZ[:, k % 2, j:j + 2, :].rearrange("p n s -> p (n s)"), pair(chunk(a, k), j // 2))
                        last.then_inc(S["z_bn"], 1)
                    if r := item(b, t, L_STZ, IC):
                        a, k = r
                        dve.wait_ge(S["z_bn"], cnt(a, NI, IC * k + IC))
                        ve.tensor_scalar(vZ[:, :], stZ[:, k % 2, :, 2], 1.0 / W, EPS_T, ALU.mult, ALU.add).then_inc(S["z_var"], 1)
                    if r := item(b, t, L_MAX, SI):
                        a, s = r
                        q = a[0] % 2
                        dve.wait_ge(S["lt_done"], cnt(a, NI, SI * s + SI))
                        if s == 0:
                            wait(dve, S["cross"], cnt(a, 1, -1))
                        dve.sem_inc(S["tick"], 1)
                        ve.max(CD[:, q, s * K:(s + 1) * K], LTS[:, s % 2, :]).then_inc(S["seg_v"], 1)
                    if (r := item(b, t, L_MAXI, SI)):
                        a, s = r
                        q = a[0] % 2
                        dve.wait_ge(S["seg_v"], cnt(a, NS, s + 1))
                        dve.sem_inc(S["tick"], 1)
                        ve.max_index(CI[:, q, s * K:(s + 1) * K], CD[:, q, s * K:(s + 1) * K], LTS[:, s % 2, :]).then_inc(S["seg_i"], 1)
                        ve.tensor_scalar(NM[:, q, s:s + 1], CD[:, q, s * K:s * K + 1], -1.0, None, ALU.mult).then_inc(S["seg_nm"], 1)
                    if (r := item(b, t, S_CAND, NI)):
                        a, _ = r
                        q = a[0] % 2
                        dve.wait_ge(S["seg_i"], cnt(a, NS, NS))
                        ve.tensor_scalar(ci[:, 0, :], CI[:, q, :], P - 1, 7, ALU.bitwise_and, ALU.logical_shift_left)
                        ve.tensor_scalar(ci[:, 1, :], CI[:, q, :], 7, 1, ALU.logical_shift_right, ALU.logical_shift_left).then_inc(S["c1"], 1)
                        dve.wait_ge(S["c1"], cnt(a, 2, 1))
                        tk = CD[:, q, NS * K:2 * NS * K]
                        ve.tensor_tensor(tk, ci[:, 0, :], ci[:, 1, :], ALU.add).then_inc(S["c1"], 1)
                        dve.wait_ge(S["c1"], cnt(a, 2, 2))
                        ve.tensor_tensor(tk, tk, soff[:, :], ALU.add).then_inc(S["cand"], 1)
                    if (r := item(b, t, S_TOP + 1, NI)):
                        a, _ = r
                        M = 2 * NS * K
                        dve.wait_ge(S["t1"], cnt(a, 4, 4))
                        xt = XT[:, :, :].rearrange("p g n -> p (g n)").unsqueeze(1).to_broadcast([P, K, M])
                        ve.tensor_tensor(hot[:, :, :], hot[:, :, :], xt, ALU.mult).then_inc(S["t2"], 1)
                        dve.wait_ge(S["t2"], cnt(a, 5, 1))
                        ve.tensor_reduce(tok8[:, :], hot[:, :, :], AX, ALU.add).then_inc(S["t2"], 1)
                    if (r := item(b, t, S_FIN, NI)):
                        a, _ = r
                        dve.wait_ge(S["texp"], cnt(a, 1, 1))
                        ve.tensor_tensor(sm[:, 2:2 + 2 * NS], eL[:, :, :].rearrange("p g n -> p (g n)"),
                                         XS[:, :, :].rearrange("p g n -> p (g n)"), ALU.mult).then_inc(S["t2"], 1)
                        dve.wait_ge(S["t2"], cnt(a, 5, 3))
                        ve.tensor_reduce(sm[:, 0:1], sm[:, 2:2 + 2 * NS], AX, ALU.add).then_inc(S["t2"], 1)
                        dve.wait_ge(S["t2"], cnt(a, 5, 4))
                        ve.reciprocal(sm[:, 1:2], sm[:, 0:1]).then_inc(S["t2"], 1)
                        dve.wait_ge(S["t2"], cnt(a, 5, 5))
                        bv = val(a)
                        for g in range(2):
                            h = slice(g * E, (g + 1) * E)
                            ve.tensor_scalar(TV[h, bass.ds(bv * 4, 4)], e8[h, g * 4:g * 4 + 4], sm[h, 1:2], None, ALU.mult)
                            last = ve.tensor_copy(TK[h, bass.ds(bv * 4, 4)], tok8[h, g * 4:g * 4 + 4])
                        last.then_inc(S["fin"], 1)
                    if (n := late(b, t, S_GATH)) is not None:
                        if n == 0:
                            dve.wait_ge(s_prep, 4)
                            ve.tensor_tensor(fold, ident[:, 0:E], ident[:, E:2 * E], ALU.add)
                        dve.wait_ge(S["fin"], n + 1)
                        ve.tensor_scalar(rowf[:, n, :], TK[:, n * 4:n * 4 + 4], boff[:, n:n + 1], None, ALU.add).then_inc(R_["rowf"], 1)
                        dve.wait_ge(R_["rowf"], n + 1)
                        ve.tensor_copy(idx[:, n, :], rowf[:, n, :]).then_inc(R_["idx"], 1)
                    if (n := late(b, t, S_POOL)) is not None:
                        q = n % 2
                        ve.tensor_tensor(D[:, q, :, :], ident[:, :].unsqueeze(1).to_broadcast([P, 4, P]),
                                         TK[:, n * 4:n * 4 + 4].unsqueeze(2).to_broadcast([P, 4, P]), ALU.mult).then_inc(R_["diag"], 1)
                        dve.wait_ge(s_rows[n % 4], n // 4 * 64 + 64)
                        for m in range(2):
                            last = ve.bn_stats(stR[:, q, 2 * m:2 * m + 2, :].rearrange("p n s -> p (n s)"),
                                               R[:, n, 2 * m:2 * m + 2, :].rearrange("p h w -> p w h"))
                        last.then_inc(R_["rbn"], 1)
                        dve.wait_ge(R_["rbn"], n + 1)
                        ve.tensor_scalar(vR[:, q, :], stR[:, q, :, 2], 1.0 / W, EPS_T, ALU.mult, ALU.add).then_inc(R_["rvar"], 1)
                        ve.tensor_tensor(R[:, n, :, :], R[:, n, :, :], stR[:, q, :, 1].unsqueeze(2).to_broadcast([P, 4, W]),
                                         ALU.subtract).then_inc(R_["cen"], 1)
                        dve.wait_ge(R_["rr"], n + 1)
                        ve.tensor_tensor(wvb[:, q, :], TV[:, n * 4:n * 4 + 4], rR[:, q, :], ALU.mult).then_inc(R_["wv"], 1)
                        dve.wait_ge(R_["wv"], n + 1)
                        wait(dve, R_["pmm"], n - 1)
                        ve.tensor_tensor(FW[:, q, :, :], fold.unsqueeze(1).to_broadcast([P, 4, E]),
                                         wvb[:, q, :].unsqueeze(2).to_broadcast([P, 4, E]), ALU.mult).then_inc(R_["fw"], 1)
                    if (n := late(b, t, S_POOL + 1)) is not None:
                        q = n % 2
                        dve.wait_ge(R_["row"], n + 1)
                        ve.tensor_tensor(EQ[:, n, :, :], (G, O[2])[n % 2][:, :].rearrange("p (j w) -> p j w", j=4),
                                         TK[:, n * 4:n * 4 + 4].unsqueeze(2).to_broadcast([P, 4, P]), ALU.is_equal).then_inc(R_["eq"], 1)
                        dve.wait_ge(R_["eq"], n + 1)
                        ve.tensor_tensor(first[:, q, :, :], EQ[:, n, :, :], before.unsqueeze(1).to_broadcast([P, 4, P]),
                                         ALU.mult).then_inc(R_["fst"], 1)
                        dve.wait_ge(R_["fst"], n + 1)
                        ve.tensor_reduce(nfirst[:, q, :], first[:, q, :, :], AX, ALU.add).then_inc(R_["nf"], 1)
                        dve.wait_ge(R_["nf"], 2 * n + 1)
                        ve.tensor_scalar(nfirst[:, q, :], nfirst[:, q, :], 0.5, float(1 << 20), ALU.is_gt, ALU.mult).then_inc(R_["nf"], 1)
                        dve.wait_ge(R_["nf"], 2 * n + 2)
                        ve.tensor_tensor(idxs[:, n, :], nfirst[:, q, :], rowf[:, n, :], ALU.add).then_inc(R_["idxs"], 1)

            bodies(dve, body)
            dve.wait_ge(R_["bt"], 1)
            ve.tensor_copy(b1T, G[:, 0:HC * E].rearrange("p (c e) -> p c e", e=E))
            ve.tensor_copy(b2T, G[:, HC * E:(HC + 1) * E]).then_inc(R_["btc"], 1)
            dve.wait_ge(R_["btc"], 1)

            def hidden(n, s):
                dve.wait_ge(R_["h"], n + 1)
                ve.tensor_tensor(HB[:, s % 2, :].rearrange("p (c b) -> p c b", b=NB),
                                 (G, O[2])[s % 2][:, 0:HC * NB].rearrange("p (c b) -> p c b", b=NB),
                                 b1T[:, :, bass.ds(n, 1)].to_broadcast([P, HC, NB]), ALU.add).then_inc(R_["hb"], 1)

            def output(n, s):
                dve.wait_ge(R_["o"], n + 1)
                ve.tensor_tensor(OT[:, :, :, bass.ds(n, 1)],
                                 (T0, T1)[s % 2][:, 0:NB].unsqueeze(2).unsqueeze(3).to_broadcast([P, NB, 2, 1]),
                                 b2T[:, bass.ds(n, 1)].unsqueeze(2).unsqueeze(3).to_broadcast([P, NB, 2, 1]), ALU.add).then_inc(R_["ot"], 1)

            hidden(0, 0)
            hidden(1, 1)
            output(0, 0)
            with dve.Fori(1, E // 2) as g:
                for s in range(2):
                    hidden(g * 2 + s, s)
                    output(g * 2 + s - 1, 1 - s)
            output(E - 1, 1)
            for n in range(NB):
                dve.wait_ge(R_["xt"], n + 1)
                wait(dve, R_["cmm"], n - 1)
                ve.tensor_tensor(V[:, n % 2, :, :], (T0, T1)[n % 2][:, 0:P].unsqueeze(1).to_broadcast([P, 4, W]),
                                 TV[:, n * 4:n * 4 + 4].unsqueeze(2).to_broadcast([P, 4, W]), ALU.mult).then_inc(R_["v"], 1)


_INS = ["x", "L0_conv_wq", "L0_conv_bq", "L0_conv_wk", "L0_conv_bk", "L0_conv_wv", "L0_conv_wo", "L0_conv_gamma",
        "L0_conv_beta", "L0_ffn_gate_w", "L0_ffn_gate_b", "L0_ffn_weight1", "L0_ffn_weight2"]


def kernel(**inputs):
    import numpy as np
    import concourse.bacc as bacc
    from concourse.bass_utils import run_bass_kernel_spmd as run

    nc = bacc.Bacc("TRN2", target_bir_lowering=False, num_devices=1)
    arrays, args = {}, []
    for name in _INS:
        a = np.ascontiguousarray(inputs[name])
        arrays[f"in_{name}"] = a
        args.append(nc.dram_tensor(f"in_{name}", a.shape, F32, kind="ExternalInput").ap())
    shape = inputs["x"].shape
    args.append(nc.dram_tensor("out_dram", shape, F32, kind="ExternalOutput").ap())
    program(nc, *args)
    r = run(nc, [arrays], core_ids=[0])
    return r.results[0]["out_dram"]
```
